# Optimizing a Trainium2 kernel written in Bass

```python
import numpy as np
import jax
import jax.numpy as jnp

def _softmax(x, axis=-1):
    return jax.nn.softmax(x, axis=axis)

def _gelu(x):
    return jax.nn.gelu(x, approximate=True)

def _silu(x):
    return jax.nn.silu(x)

def _sigmoid(x):
    return jax.nn.sigmoid(x)

def _layernorm(x, axis=-1, eps=1e-05):
    m = jnp.mean(x, axis=axis, keepdims=True)
    v = jnp.var(x, axis=axis, keepdims=True)
    return (x - m) / jnp.sqrt(v + eps)

def _scatter_add(tgt, idx, src, axis=0):
    return tgt.at[idx].add(src)

def _segment_sum(src, seg, n):
    return jax.ops.segment_sum(src, seg, n)
kernel_name = 'mk_conv_seq_d1_conv_nchw256_r2_f9725c'

def setup_inputs(seed: int=0):
    np.random.seed(seed)
    _w = jnp.asarray

    def _rec_inputs():
        import jax
        import jax.numpy as jnp
        _gk = jax.random.key(seed)
        x = -0.0002928 + 1 * jax.random.normal(jax.random.fold_in(_gk, 1), (4, 128, 32, 32), jnp.float32)
        return x
    x = _rec_inputs()

    def _L0_conv_setup():
        import jax, jax.numpy as jnp
        import numpy as np
        DIM = 128
        GROUPS = 32
        EPS = 1e-06
        key = jax.random.key(seed)
        ks = jax.random.split(key, 7)
        B, C, H, W = (4, DIM, 32, 32)
        s = 1.0 / np.sqrt(C)
        return {'x': jax.random.normal(ks[0], (B, C, H, W), dtype=jnp.float32), 'gamma': jnp.ones((C,), dtype=jnp.float32), 'beta': jnp.zeros((C,), dtype=jnp.float32), 'w_qkv': jax.random.normal(ks[1], (3 * C, C), dtype=jnp.float32) * s, 'b_qkv': jnp.zeros((3 * C,), dtype=jnp.float32), 'w_proj': jax.random.normal(ks[2], (C, C), dtype=jnp.float32) * s, 'b_proj': jnp.zeros((C,), dtype=jnp.float32)}
    _L0_conv_all = _L0_conv_setup()
    _L0_conv_in = {k: v for k, v in _L0_conv_all.items() if k in ('gamma', 'beta', 'w_qkv', 'b_qkv', 'w_proj', 'b_proj')}
    del _L0_conv_all
    return {'x': x, 'L0_conv_gamma': _L0_conv_in['gamma'], 'L0_conv_beta': _L0_conv_in['beta'], 'L0_conv_w_qkv': _L0_conv_in['w_qkv'], 'L0_conv_b_qkv': _L0_conv_in['b_qkv'], 'L0_conv_w_proj': _L0_conv_in['w_proj'], 'L0_conv_b_proj': _L0_conv_in['b_proj']}

def reference(x, L0_conv_gamma, L0_conv_beta, L0_conv_w_qkv, L0_conv_b_qkv, L0_conv_w_proj, L0_conv_b_proj):
    import jax
    import jax.numpy as jnp

    def _L0_conv_ref(x, gamma, beta, w_qkv, b_qkv, w_proj, b_proj):
        import jax, jax.numpy as jnp
        import numpy as np
        DIM = 128
        GROUPS = 32
        EPS = 1e-06
        B, C, H, W = x.shape
        N = H * W
        scale = jnp.asarray(C, x.dtype) ** 0.5
        h = x.reshape(B, GROUPS, C // GROUPS, N)
        mu = h.mean(axis=(2, 3), keepdims=True)
        var = h.var(axis=(2, 3), keepdims=True)
        h = (h - mu) * jax.lax.rsqrt(var + EPS)
        h = h.reshape(B, C, N) * gamma[None, :, None] + beta[None, :, None]
        qkv = jnp.einsum('oc,bcn->bon', w_qkv, h) + b_qkv[None, :, None]
        qkv = qkv.reshape(B, 3, C, N)
        q = qkv[:, 0].transpose(0, 2, 1)
        k = qkv[:, 1].transpose(0, 2, 1)
        v = qkv[:, 2].transpose(0, 2, 1)
        attn = jnp.einsum('bqc,bkc->bqk', q, k) / scale
        attn = jax.nn.softmax(attn, axis=-1)
        out = jnp.einsum('bqk,bkc->bqc', attn, v)
        out = out.transpose(0, 2, 1)
        out = jnp.einsum('oc,bcn->bon', w_proj, out) + b_proj[None, :, None]
        return x + out.reshape(B, C, H, W)

    def _gn(v, G=32, eps=1e-05):
        B_, C_, H_, W_ = v.shape
        g = v.reshape(B_, G, C_ // G, H_, W_)
        m = jnp.mean(g, axis=(2, 3, 4), keepdims=True)
        s = jnp.var(g, axis=(2, 3, 4), keepdims=True)
        return ((g - m) / jnp.sqrt(s + eps)).reshape(v.shape)

    def _ln_c(v, eps=1e-06):
        m = jnp.mean(v, axis=1, keepdims=True)
        s = jnp.var(v, axis=1, keepdims=True)
        return (v - m) / jnp.sqrt(s + eps)

    def _ln_t(v, eps=1e-05):
        m = jnp.mean(v, axis=-1, keepdims=True)
        s = jnp.var(v, axis=-1, keepdims=True)
        return (v - m) / jnp.sqrt(s + eps)

    def _to_tokens(v):
        B_, C_, H_, W_ = v.shape
        return v.reshape(B_, C_, H_ * W_).transpose(0, 2, 1)

    def _from_tokens(t, like):
        B_, C_, H_, W_ = like.shape
        return t.transpose(0, 2, 1).reshape(B_, C_, H_, W_)
    x = _L0_conv_ref(x, L0_conv_gamma, L0_conv_beta, L0_conv_w_qkv, L0_conv_b_qkv, L0_conv_w_proj, L0_conv_b_proj)
    return x

_drawn_inputs = setup_inputs


def setup_inputs(seed=0):
    import zlib

    import numpy as np

    out = dict(_drawn_inputs(seed))
    spreads = {'L0_conv_gamma': (1.0, 0.2),
     'L0_conv_beta': (0.0, 0.1),
     'L0_conv_b_qkv': (0.0, 0.1),
     'L0_conv_b_proj': (0.0, 0.1)}
    factors = {}
    for name, (base, spread) in spreads.items():
        noise = np.random.default_rng([zlib.crc32(name.encode()), seed]).standard_normal(out[name].shape)
        drawn = base * np.exp(spread * noise) if base else spread * noise
        out[name] = jnp.asarray(drawn.astype(out[name].dtype))
    for name, factor in factors.items():
        out[name] = (out[name] * factor).astype(out[name].dtype)
    return out
```

```python
from contextlib import ExitStack
import math

import concourse.bass as bass
from concourse import mybir

ALU = mybir.AluOpType
ACT = mybir.ActivationFunctionType
F32 = mybir.dt.float32
F16 = mybir.dt.float16
U32 = mybir.dt.uint32
AX_X = mybir.AxisListType.X
RMAX = bass.bass_isa.ReduceOp.max
ds = bass.ds

P = 128
B = 4
N = 1024
GROUP = 4
EPS = 1e-6
HALF = 512
TILES = N // P
CT = HALF // P
CHUNKS = N // HALF
T_LAG = 2
PV_LAG = T_LAG + CT

Z_BOUND = math.sqrt(GROUP * N)
T_MAX = 2.0
C_PER_A = T_MAX * P * Z_BOUND / T_MAX
V_MAX = 4.0
W_LOADS = 8
TINY = 1e-30
LOG2_P = 10
SUM_MAX = float(N * 2 ** LOG2_P)


def attention_block(nc, x, gamma, beta, w_qkv, b_qkv, w_proj, b_proj, out):
    x_d = x.rearrange("b c h w -> b c (h w)")
    out_d = out.rearrange("b c h w -> b c (h w)")
    col = lambda v: v.rearrange("(c a) -> c a", a=1)
    esc_factor = 1.0 / (T_MAX * math.sqrt(P))

    with ExitStack() as ctx:
        def sb(name, shape, dt=F32):
            return ctx.enter_context(nc.sbuf_tensor(name, shape, dt))

        def pb(name, shape, dt=F32):
            return ctx.enter_context(nc.psum_tensor(name, shape, dt))

        def sem(name):
            return ctx.enter_context(nc.semaphore(name))

        x_sb = sb("x_sb", [P, B * N])
        wqkv_sb = sb("wqkv_sb", [P, 3, P])
        wp_sb = sb("wp_sb", [P, P])
        gamma_c = sb("gamma_c", [P, 1])
        gamma_row = sb("gamma_row", [P, P])
        beta_c = sb("beta_c", [P, 1])
        bq_c = sb("bq_c", [P, 1])
        bv_c = sb("bv_c", [P, 1])
        bp_c = sb("bp_c", [P, 1])
        ident32 = sb("ident32", [P, P])
        ident16 = sb("ident16", [P, P], F16)
        ones16 = sb("ones16", [P, P], F16)
        zero32 = sb("zero32", [P, P])
        group_avg = sb("group_avg", [P, P])
        group_sum = sb("group_sum", [P, P // GROUP])
        minus_half = sb("minus_half", [P, 1])
        wpT = sb("wpT", [P, P])
        a_raw = sb("a_raw", [P, P])
        w_raw = sb("w_raw", [P, P])
        a_mat = sb("a_mat", [P, P])
        w_mat = sb("w_mat", [P, P])
        c_raw = sb("c_raw", [P, 1])
        c_abs = sb("c_abs", [P, 1])
        ct = sb("ct", [P, 1])
        bo = sb("bo", [P, 1])
        wmax = sb("wmax", [P, 3])
        wmax_p = sb("wmax_p", [P, 2])
        wmax_all = sb("wmax_all", [P, 2])
        wmax_safe = sb("wmax_safe", [P, 2])
        winv = sb("winv", [P, 2])
        a_scaled = sb("a_scaled", [P, P])
        w_scaled = sb("w_scaled", [P, P])
        a_hi = sb("a_hi", [P, P], F16)
        a_lo = sb("a_lo", [P, P], F16)
        w_hi = sb("w_hi", [P, P], F16)
        w_lo = sb("w_lo", [P, P], F16)
        esc = sb("esc", [P, 1])
        neg_esc = sb("neg_esc", [P, 1])
        o_scale = sb("o_scale", [P, 1])
        bn = sb("bn", [P, 2, 6])
        bn_seen = sb("bn_seen", [P, 2])
        chan_mv = sb("chan_mv", [P, 2])
        dev = sb("dev", [P, 1])
        var_in = sb("var_in", [P, 1])
        mean_g = sb("mean_g", [P, 1])
        var_eps = sb("var_eps", [P, 1])
        rstd = sb("rstd", [P, 1])
        z32 = sb("z32", [P, N])
        z_hi = sb("z_hi", [P, B * N], F16)
        z_lo = sb("z_lo", [P, B * N], F16)
        t_hi = sb("t_hi", [P, B * N], F16)
        t_lo = sb("t_lo", [P, B * N], F16)
        v_hi = sb("v_hi", [P, B * N], F16)
        v_lo = sb("v_lo", [P, B * N], F16)
        row_max = sb("row_max", [P, 2])
        exp_bias = sb("exp_bias", [P, 2])
        probs = sb("probs", [P, 2, N])
        p_hi = sb("p_hi", [P, 2, N], F16)
        p_lo = sb("p_lo", [P, 2, N], F16)
        row_sum = sb("row_sum", [P, CHUNKS, CT])
        rinv = sb("rinv", [P, CT])
        r_hi = sb("r_hi", [P, CT], F16)
        r_lo = sb("r_lo", [P, CT], F16)
        diag_hi = sb("diag_hi", [P, CT, P], F16)
        diag_lo = sb("diag_lo", [P, CT, P], F16)
        ptT = sb("ptT", [P, CHUNKS, 2, TILES, HALF], F16)
        r_sb = sb("r_sb", [P, HALF])
        attn = sb("attn", [P, HALF])
        out_sb = sb("out_sb", [P, B * N])

        scores = pb("scores", [P, 2, N])
        tr = pb("tr", [P, 2, N], F16)
        pv = pb("pv", [P, HALF])
        misc = pb("misc", [P, HALF])

        x_first = sem("x_first")
        x_rest = sem("x_rest")
        w_loaded = sem("w_loaded")
        zeroed = sem("zeroed")
        consts = sem("consts")
        const_dve = sem("const_dve")
        setup_pe = sem("setup_pe")
        setup_dve = sem("setup_dve")
        max_all = sem("max_all")
        bn_done = sem("bn_done")
        chan_ready = sem("chan_ready")
        mean_psum = sem("mean_psum")
        dev_ready = sem("dev_ready")
        var_ready = sem("var_ready")
        var_psum = sem("var_psum")
        mean_ready = sem("mean_ready")
        vareps_ready = sem("vareps_ready")
        rstd_ready = sem("rstd_ready")
        z_ready = sem("z_ready")
        zhi_ready = sem("zhi_ready")
        zlo_ready = sem("zlo_ready")
        t_psum = sem("t_psum")
        thi_ready = sem("thi_ready")
        tlo_ready = sem("tlo_ready")
        v_psum = sem("v_psum")
        vhi_ready = sem("vhi_ready")
        vlo_ready = sem("vlo_ready")
        xb_ready = sem("xb_ready")
        scores_ready = sem("scores_ready")
        max_ready = sem("max_ready")
        bias_ready = sem("bias_ready")
        exp_ready = sem("exp_ready")
        phi_ready = sem("phi_ready")
        plo_ready = sem("plo_ready")
        tr_hi = sem("tr_hi")
        tr_lo = sem("tr_lo")
        ptT_hi = sem("ptT_hi")
        ptT_lo = sem("ptT_lo")
        pv_ready = sem("pv_ready")
        rinv_ready = sem("rinv_ready")
        rhi_ready = sem("rhi_ready")
        rlo_ready = sem("rlo_ready")
        diag_ready = sem("diag_ready")
        r_psum = sem("r_psum")
        r_ready = sem("r_ready")
        attn_ready = sem("attn_ready")
        out_ready = sem("out_ready")
        stored = sem("stored")

        def wait(eng, s, value):
            if not isinstance(value, int) or value > 0:
                eng.wait_ge(s, value)

        def images(eng, body):
            body(0, prev=False, cur=True, nxt=True)
            with eng.Fori(1, B - 1) as b:
                body(b, prev=True, cur=True, nxt=True)
            body(B - 1, prev=True, cur=True, nxt=False)
            body(B, prev=True, cur=False, nxt=False)

        block = ctx.enter_context(nc.Block())

        @block.sync
        def _(sp):
            for half in range(2):
                cols = slice(half * HALF, (half + 1) * HALF)
                sp.dma_start(x_sb[:, cols], x_d[0, :, cols]).then_inc(x_first, 16)
            for b in range(1, B):
                sp.dma_start(x_sb[:, b * N:(b + 1) * N], x_d[b]).then_inc(x_rest, 16)
            for h in range(B * CHUNKS):
                b, c = divmod(h, CHUNKS)
                sp.wait_ge(out_ready, h + 1)
                sp.dma_start(out_d[b, :, c * HALF:(c + 1) * HALF],
                             out_sb[:, h * HALF:(h + 1) * HALF]).then_inc(stored, 16)
            sp.wait_ge(stored, 16 * B * CHUNKS)

        @block.gpsimd
        def _(pool):
            nc.gpsimd.memset(zero32[:], 0.0).then_inc(zeroed, 1)
            pool.wait_ge(zeroed, 1)
            nc.gpsimd.affine_select(out=ident32[:], in_=zero32[:], compare_op=ALU.not_equal, fill=1.0, base=0,
                                    pattern=[[-1, P]], channel_multiplier=1).then_inc(consts, 1)
            def power(b):
                pool.wait_ge(vareps_ready, b + 1)
                nc.gpsimd.tensor_tensor(rstd[:], var_eps[:], minus_half[:], ALU.pow).then_inc(rstd_ready, 1)

            def z_low(b):
                pool.wait_ge(z_ready, b + 1)
                pool.wait_ge(zhi_ready, b + 1)
                nc.gpsimd.tensor_tensor(z_lo[:, ds(b * N, N)], z32[:], z_hi[:, ds(b * N, N)],
                                        ALU.subtract).then_inc(zlo_ready, 1)

            def p_low(b, s):
                g = b * TILES + s
                pool.wait_ge(exp_ready, g + 1)
                pool.wait_ge(phi_ready, g + 1)
                wait(pool, tr_lo, g - 1)
                nc.gpsimd.tensor_tensor(p_lo[:, s % 2], probs[:, s % 2], p_hi[:, s % 2],
                                        ALU.subtract).then_inc(plo_ready, 1)

            def residual(b, c):
                h = b * CHUNKS + c
                pool.wait_ge(attn_ready, h + 1)
                pool.wait_ge(xb_ready, b + 1)
                cols = ds(b * N + c * HALF, HALF)
                nc.gpsimd.tensor_tensor(out_sb[:, cols], attn[:], x_sb[:, cols], ALU.add).then_inc(out_ready, 1)

            power(0)
            pool.wait_ge(setup_dve, 9)
            nc.gpsimd.partition_all_reduce(wmax_all[:], wmax_p[:], P, RMAX).then_inc(max_all, 1)
            z_low(0)

            def body(b, prev, cur, nxt):
                for s in range(TILES):
                    if cur:
                        p_low(b, s)
                    if prev and s in (2, 6):
                        residual(b - 1, s // CT)
                    if nxt and s == 3:
                        power(b + 1)
                    if nxt and s == 4:
                        z_low(b + 1)

            images(pool, body)

        @block.scalar
        def _(act):
            act.dma_start(wqkv_sb[:], w_qkv.rearrange("(t o) c -> o t c", t=3)).then_inc(w_loaded, 16)
            act.dma_start(wp_sb[:], w_proj).then_inc(w_loaded, 16)
            act.dma_start(gamma_c[:], col(gamma)).then_inc(w_loaded, 16)
            act.dma_start(beta_c[:], col(beta)).then_inc(w_loaded, 16)
            act.dma_start(bq_c[:], col(b_qkv[0:P])).then_inc(w_loaded, 16)
            act.dma_start(bv_c[:], col(b_qkv[2 * P:3 * P])).then_inc(w_loaded, 16)
            act.dma_start(bp_c[:], col(b_proj)).then_inc(w_loaded, 16)
            act.dma_start(gamma_row[:], gamma.rearrange("(a c) -> a c", a=1).broadcast_to([P, P])
                          ).then_inc(w_loaded, 16)

            def z_high(b):
                act.wait_ge(z_ready, b + 1)
                nc.scalar.activation(z_hi[:, ds(b * N, N)], z32[:], ACT.Copy).then_inc(zhi_ready, 1)

            def t_high(b, half):
                act.wait_ge(t_psum, b * 2 + half + 1)
                if half == 0:
                    act.wait_ge(setup_dve, 22)
                nc.scalar.activation(t_hi[:, ds(b * N + half * HALF, HALF)], misc[:], ACT.Identity,
                                     bias=ct[:]).then_inc(thi_ready, 1)

            def v_high(b, half):
                act.wait_ge(v_psum, b * 2 + half + 1)
                nc.scalar.activation(v_hi[:, ds(b * N + half * HALF, HALF)], misc[:], ACT.Copy
                                     ).then_inc(vhi_ready, 1)

            def exponentials(b, s):
                g = b * TILES + s
                act.wait_ge(bias_ready, g + 1)
                wait(act, plo_ready, g - 1)
                if s % CT == 0:
                    wait(act, rinv_ready, b * CHUNKS + s // CT - 1)
                nc.scalar.activation(probs[:, s % 2], scores[:, s % 2], ACT.Exp, bias=exp_bias[:, s % 2:s % 2 + 1],
                                     scale=esc[:], accum_out=row_sum[:, s // CT, s % CT:s % CT + 1]
                                     ).then_inc(exp_ready, 1)
                act.wait_ge(exp_ready, g + 1)
                wait(act, tr_hi, g - 1)
                nc.scalar.activation(p_hi[:, s % 2], probs[:, s % 2], ACT.Copy).then_inc(phi_ready, 1)

            def r_copy(b, c):
                h = b * CHUNKS + c
                act.wait_ge(r_psum, h + 1)
                wait(act, attn_ready, h)
                nc.scalar.activation(r_sb[:], misc[:], ACT.Copy).then_inc(r_ready, 1)

            z_high(0)
            t_high(0, 0)
            t_high(0, 1)

            def body(b, prev, cur, nxt):
                for s in range(TILES):
                    if cur:
                        exponentials(b, s)
                    if cur and s == 0:
                        v_high(b, 0)
                    if prev and s in (1, 5):
                        r_copy(b - 1, s // CT)
                    if cur and s == 2:
                        nc.scalar.activation(x_sb[:, ds(b * N, N)], x_sb[:, ds(b * N, N)], ACT.Identity,
                                             bias=bo[:]).then_inc(xb_ready, 1)
                    if cur and s == 4:
                        v_high(b, 1)
                    if nxt and s == 4:
                        z_high(b + 1)
                    if nxt and s in (6, 7):
                        t_high(b + 1, s - 6)

            images(act, body)

        @block.vector
        def _(dve):
            nc.vector.memset(minus_half[:], -0.5).then_inc(const_dve, 1)
            nc.vector.memset(ones16[:], 1.0).then_inc(const_dve, 1)
            dve.wait_ge(consts, 1)
            nc.vector.tensor_copy(ident16[:], ident32[:]).then_inc(const_dve, 1)
            nc.vector.tensor_reduce(group_sum[:], ident32[:].rearrange("p (g j) -> p g j", j=GROUP),
                                    AX_X, ALU.add).then_inc(const_dve, 1)
            dve.wait_ge(const_dve, 4)
            nc.vector.tensor_scalar(group_avg[:].rearrange("p (g j) -> p g j", j=GROUP),
                                    group_sum[:].unsqueeze(2).broadcast_to([P, P // GROUP, GROUP]),
                                    1.0 / GROUP, None, ALU.mult).then_inc(const_dve, 1)

            def channel_stats(b):
                if isinstance(b, int) and b == 0:
                    dve.wait_ge(x_first, 32)
                else:
                    dve.wait_ge(x_rest, 16 * (B - 1))
                for half in range(2):
                    nc.vector.bn_stats(bn[:, half, :], x_sb[:, ds(b * N + half * HALF, HALF)]).then_inc(bn_done, 1)
                dve.wait_ge(bn_done, b * 2 + 2)
                nc.vector.tensor_copy(bn_seen[:], bn[:, :, 0])
                nc.vector.bn_aggr(chan_mv[:], bn[:].rearrange("p a f -> p (a f)")).then_inc(chan_ready, 1)

            def group_mean(b):
                dve.wait_ge(mean_psum, b + 1)
                dve.wait_ge(chan_ready, b + 1)
                nc.vector.tensor_tensor(dev[:], chan_mv[:, 0:1], misc[:, 0:1], ALU.subtract).then_inc(dev_ready, 1)
                dve.wait_ge(dev_ready, b + 1)
                nc.vector.scalar_tensor_tensor(out=var_in[:], in0=dev[:], scalar=dev[:], in1=chan_mv[:, 1:2],
                                               op0=ALU.mult, op1=ALU.add).then_inc(var_ready, 1)
                nc.vector.tensor_tensor(mean_g[:], chan_mv[:, 0:1], dev[:], ALU.subtract).then_inc(mean_ready, 1)

            def group_var(b):
                dve.wait_ge(var_psum, b + 1)
                nc.vector.tensor_scalar(var_eps[:], misc[:, 0:1], EPS, None, ALU.add).then_inc(vareps_ready, 1)

            def normalise(b):
                dve.wait_ge(rstd_ready, b + 1)
                dve.wait_ge(mean_ready, b + 1)
                wait(dve, zlo_ready, b)
                wait(dve, zhi_ready, b)
                nc.vector.tensor_scalar(z32[:], x_sb[:, ds(b * N, N)], mean_g[:], rstd[:], ALU.subtract, ALU.mult
                                        ).then_inc(z_ready, 1)

            def t_low(b, half):
                dve.wait_ge(thi_ready, b * 2 + half + 1)
                cols = ds(b * N + half * HALF, HALF)
                nc.vector.scalar_tensor_tensor(out=t_lo[:, cols], in0=misc[:], scalar=ct[:], in1=t_hi[:, cols],
                                               op0=ALU.add, op1=ALU.subtract).then_inc(tlo_ready, 1)

            def v_low(b, half):
                dve.wait_ge(vhi_ready, b * 2 + half + 1)
                cols = ds(b * N + half * HALF, HALF)
                nc.vector.tensor_tensor(v_lo[:, cols], misc[:], v_hi[:, cols], ALU.subtract).then_inc(vlo_ready, 1)

            def maxima(b, s):
                g = b * TILES + s
                dve.wait_ge(scores_ready, g + 1)
                nc.vector.tensor_reduce(row_max[:, s % 2:s % 2 + 1], scores[:, s % 2], AX_X, ALU.max
                                        ).then_inc(max_ready, 1)
                dve.wait_ge(max_ready, g + 1)
                wait(dve, exp_ready, g - 1)
                nc.vector.tensor_scalar(exp_bias[:, s % 2:s % 2 + 1], row_max[:, s % 2:s % 2 + 1], neg_esc[:],
                                        LOG2_P * math.log(2.0), ALU.mult, ALU.add).then_inc(bias_ready, 1)

            def take_transposes(b, i):
                g = b * TILES + i
                c, j = divmod(i, CT)
                h = b * CHUNKS + c
                if j == 0:
                    wait(dve, pv_ready, h - CHUNKS + 1)
                for part, (ready, taken) in enumerate(((tr_hi, ptT_hi), (tr_lo, ptT_lo))):
                    dve.wait_ge(ready, g + 1)
                    nc.vector.tensor_copy(
                        ptT[:, c, part, :, j * P:(j + 1) * P].bitcast(U32),
                        tr[:, part].bitcast(U32).rearrange("p (k q) -> p k q", k=TILES)).then_inc(taken, 1)

            def inverse_sums(b, c):
                h = b * CHUNKS + c
                dve.wait_ge(exp_ready, b * TILES + (c + 1) * CT)
                nc.vector.reciprocal(rinv[:], row_sum[:, c]).then_inc(rinv_ready, 1)
                dve.wait_ge(rinv_ready, h + 1)
                nc.vector.tensor_scalar(r_hi[:], rinv[:], SUM_MAX, None, ALU.mult).then_inc(rhi_ready, 1)
                dve.wait_ge(rhi_ready, h + 1)
                nc.vector.scalar_tensor_tensor(out=r_lo[:], in0=rinv[:], scalar=SUM_MAX, in1=r_hi[:],
                                               op0=ALU.mult, op1=ALU.subtract).then_inc(rlo_ready, 1)
                wait(dve, r_psum, h)
                dve.wait_ge(rlo_ready, h + 1)
                eye = ident16[:].unsqueeze(1).broadcast_to([P, CT, P])
                for diag, r in ((diag_hi, r_hi), (diag_lo, r_lo)):
                    nc.vector.tensor_tensor(diag[:], eye, r[:].unsqueeze(2).broadcast_to([P, CT, P]), ALU.mult
                                            ).then_inc(diag_ready, 1)

            def scale_output(b, c):
                h = b * CHUNKS + c
                dve.wait_ge(pv_ready, h + 1)
                dve.wait_ge(r_ready, h + 1)
                wait(dve, out_ready, h)
                nc.vector.scalar_tensor_tensor(out=attn[:], in0=pv[:], scalar=o_scale[:], in1=r_sb[:],
                                               op0=ALU.mult, op1=ALU.mult).then_inc(attn_ready, 1)

            channel_stats(0)

            dve.wait_ge(w_loaded, 16 * W_LOADS)
            dve.wait_ge(setup_pe, 1)
            nc.vector.tensor_copy(wpT[:], scores[:, 0, 0:P]).then_inc(setup_dve, 1)
            dve.wait_ge(setup_pe, 2)
            nc.vector.tensor_copy(a_raw[:], scores[:, 0, HALF:HALF + P]).then_inc(setup_dve, 1)
            nc.vector.scalar_tensor_tensor(out=a_mat[:], in0=scores[:, 0, HALF:HALF + P], scalar=gamma_c[:],
                                           in1=gamma_row[:], op0=ALU.mult, op1=ALU.mult).then_inc(setup_dve, 1)
            group_mean(0)
            dve.wait_ge(setup_pe, 3)
            nc.vector.tensor_copy(w_raw[:], scores[:, 1, 0:P]).then_inc(setup_dve, 1)
            nc.vector.tensor_scalar(w_mat[:], scores[:, 1, 0:P], gamma_c[:], None, ALU.mult).then_inc(setup_dve, 1)
            group_var(0)
            dve.wait_ge(setup_dve, 5)
            nc.vector.tensor_reduce(wmax[:, 0:1], a_mat[:], AX_X, ALU.max, apply_absolute_value=True
                                    ).then_inc(setup_dve, 1)
            nc.vector.tensor_reduce(wmax_p[:, 1:2], w_mat[:], AX_X, ALU.max, apply_absolute_value=True
                                    ).then_inc(setup_dve, 1)
            dve.wait_ge(setup_pe, 4)
            nc.vector.tensor_scalar(c_raw[:], scores[:, 1, HALF:HALF + 1], gamma_c[:], None, ALU.mult
                                    ).then_inc(setup_dve, 1)
            dve.wait_ge(setup_dve, 8)
            nc.vector.tensor_reduce(c_abs[:], c_raw[:], AX_X, ALU.max, apply_absolute_value=True
                                    ).then_inc(const_dve, 1)
            dve.wait_ge(const_dve, 6)
            nc.vector.scalar_tensor_tensor(out=wmax_p[:, 0:1], in0=c_abs[:], scalar=1.0 / C_PER_A, in1=wmax[:, 0:1],
                                           op0=ALU.mult, op1=ALU.max).then_inc(setup_dve, 1)
            normalise(0)
            dve.wait_ge(setup_pe, 5)
            nc.vector.tensor_tensor(bo[:], bp_c[:], pv[:, 0:1], ALU.add).then_inc(setup_dve, 1)
            dve.wait_ge(max_all, 1)
            nc.vector.tensor_scalar(wmax_safe[:], wmax_all[:], TINY, None, ALU.max).then_inc(setup_dve, 1)
            dve.wait_ge(setup_dve, 11)
            nc.vector.reciprocal(winv[:], wmax_safe[:]).then_inc(setup_dve, 1)
            nc.vector.tensor_scalar(esc[:], wmax_safe[:, 0:1], esc_factor, None, ALU.mult).then_inc(setup_dve, 1)
            nc.vector.tensor_scalar(neg_esc[:], wmax_safe[:, 0:1], -esc_factor, None, ALU.mult).then_inc(setup_dve, 1)
            nc.vector.tensor_scalar(o_scale[:], wmax_safe[:, 1:2], 1.0 / (V_MAX * SUM_MAX), None, ALU.mult
                                    ).then_inc(setup_dve, 1)
            dve.wait_ge(setup_dve, 15)
            nc.vector.tensor_scalar(a_scaled[:], a_mat[:], winv[:, 0:1], T_MAX, ALU.mult, ALU.mult
                                    ).then_inc(setup_dve, 1)
            nc.vector.tensor_scalar(w_scaled[:], w_mat[:], winv[:, 1:2], V_MAX, ALU.mult, ALU.mult
                                    ).then_inc(setup_dve, 1)
            nc.vector.tensor_scalar(ct[:], c_raw[:], winv[:, 0:1], T_MAX, ALU.mult, ALU.mult).then_inc(setup_dve, 1)
            dve.wait_ge(setup_dve, 18)
            nc.vector.tensor_copy(a_hi[:], a_scaled[:]).then_inc(setup_dve, 1)
            nc.vector.tensor_copy(w_hi[:], w_scaled[:]).then_inc(setup_dve, 1)
            dve.wait_ge(setup_dve, 20)
            nc.vector.tensor_tensor(a_lo[:], a_scaled[:], a_hi[:], ALU.subtract).then_inc(setup_dve, 1)
            nc.vector.tensor_tensor(w_lo[:], w_scaled[:], w_hi[:], ALU.subtract).then_inc(setup_dve, 1)

            t_low(0, 0)
            t_low(0, 1)

            def body(b, prev, cur, nxt):
                for s in range(TILES):
                    if cur:
                        maxima(b, s)
                    if prev and s < T_LAG:
                        take_transposes(b - 1, s + TILES - T_LAG)
                    if cur and s >= T_LAG:
                        take_transposes(b, s - T_LAG)
                    if prev and s in (0, 4):
                        inverse_sums(b - 1, s // CT)
                    if cur and s == 0:
                        v_low(b, 0)
                    if nxt and s == 1:
                        channel_stats(b + 1)
                    if prev and s in (1, 5):
                        scale_output(b - 1, s // CT)
                    if nxt and s == 2:
                        group_mean(b + 1)
                    if nxt and s == 3:
                        group_var(b + 1)
                        normalise(b + 1)
                    if cur and s == 4:
                        v_low(b, 1)
                    if nxt and s in (6, 7):
                        t_low(b + 1, s - 6)

            images(dve, body)

        @block.tensor
        def _(pe):
            def group_average(b, source, value, done):
                pe.wait_ge(source, b + 1)
                nc.tensor.matmul(misc[:, 0:1], group_avg[:], value, start=True, stop=True).then_inc(done, 1)

            def t_products(b, half):
                pe.wait_ge(zlo_ready, b + 1)
                if half:
                    pe.wait_ge(tlo_ready, b * 2 + 1)
                cols = ds(b * N + half * HALF, HALF)
                nc.tensor.matmul(misc[:], a_hi[:], z_hi[:, cols], start=True, stop=False)
                nc.tensor.matmul(misc[:], a_hi[:], z_lo[:, cols], start=False, stop=False)
                nc.tensor.matmul(misc[:], a_lo[:], z_hi[:, cols], start=False, stop=True).then_inc(t_psum, 1)

            def v_products(b, half):
                for k in range(CT):
                    cols = ds(b * N + (half * CT + k) * P, P)
                    dst = misc[:, k * P:(k + 1) * P]
                    nc.tensor.matmul(dst, z_hi[:, cols], w_hi[:], start=True, stop=False)
                    nc.tensor.matmul(dst, z_hi[:, cols], w_lo[:], start=False, stop=False)
                    last = nc.tensor.matmul(dst, z_lo[:, cols], w_hi[:], start=False, stop=True)
                last.then_inc(v_psum, 1)

            def score_tile(b, s):
                g = b * TILES + s
                pe.wait_ge(tlo_ready, b * 2 + s // CT + 1)
                wait(pe, exp_ready, g - 1)
                rows = ds(b * N + s * P, P)
                for half in range(2):
                    cols = ds(b * N + half * HALF, HALF)
                    dst = scores[:, s % 2, half * HALF:(half + 1) * HALF]
                    nc.tensor.matmul(dst, t_hi[:, rows], z_hi[:, cols], start=True, stop=False)
                    nc.tensor.matmul(dst, t_hi[:, rows], z_lo[:, cols], start=False, stop=False)
                    last = nc.tensor.matmul(dst, t_lo[:, rows], z_hi[:, cols], start=False, stop=True)
                last.then_inc(scores_ready, 1)

            def transposes(b, i):
                g = b * TILES + i
                for part, (src, ready, taken, done) in enumerate(((p_hi, phi_ready, ptT_hi, tr_hi),
                                                                  (p_lo, plo_ready, ptT_lo, tr_lo))):
                    pe.wait_ge(ready, g + 1)
                    wait(pe, taken, g)
                    for k in range(TILES):
                        last = nc.tensor.transpose(tr[:, part, k * P:(k + 1) * P],
                                                   src[:, i % 2, k * P:(k + 1) * P], ident16[:])
                    last.then_inc(done, 1)

            def pv_quarter(b, r):
                c, quarter = divmod(r, CT)
                h = b * CHUNKS + c
                if quarter == 0:
                    pe.wait_ge(ptT_hi, b * TILES + (c + 1) * CT)
                    pe.wait_ge(ptT_lo, b * TILES + (c + 1) * CT)
                    wait(pe, attn_ready, h)
                if c == 0 and quarter % 2 == 0:
                    pe.wait_ge(vlo_ready, b * 2 + quarter // 2 + 1)
                per = TILES // CT
                for k in range(quarter * per, (quarter + 1) * per):
                    keys = ds(b * N + k * P, P)
                    nc.tensor.matmul(pv[:], v_hi[:, keys], ptT[:, c, 0, k], start=(k == 0), stop=False)
                    nc.tensor.matmul(pv[:], v_hi[:, keys], ptT[:, c, 1, k], start=False, stop=False)
                    last = nc.tensor.matmul(pv[:], v_lo[:, keys], ptT[:, c, 0, k], start=False,
                                            stop=(k == TILES - 1))
                if quarter == CT - 1:
                    last.then_inc(pv_ready, 1)

            def spread_inverse(b, c):
                h = b * CHUNKS + c
                pe.wait_ge(diag_ready, 2 * h + 2)
                nc.tensor.matmul(misc[:], ones16[:], diag_hi[:].rearrange("p a b -> p (a b)"), start=True, stop=False)
                nc.tensor.matmul(misc[:], ones16[:], diag_lo[:].rearrange("p a b -> p (a b)"), start=False, stop=True
                                 ).then_inc(r_psum, 1)

            pe.wait_ge(consts, 1)
            pe.wait_ge(w_loaded, 16 * W_LOADS)
            nc.tensor.transpose(scores[:, 0, 0:P], wp_sb[:], ident32[:]).then_inc(setup_pe, 1)
            nc.tensor.matmul(scores[:, 0, HALF:HALF + P], wqkv_sb[:, 0], wqkv_sb[:, 1], start=True, stop=True
                             ).then_inc(setup_pe, 1)
            pe.wait_ge(const_dve, 5)
            group_average(0, chan_ready, chan_mv[:, 0:1], mean_psum)
            pe.wait_ge(setup_dve, 1)
            nc.tensor.matmul(scores[:, 1, 0:P], wqkv_sb[:, 2], wpT[:], start=True, stop=True).then_inc(setup_pe, 1)
            group_average(0, var_ready, var_in[:], var_psum)
            pe.wait_ge(setup_dve, 2)
            nc.tensor.matmul(scores[:, 1, HALF:HALF + 1], a_raw[:], beta_c[:], start=True, stop=False)
            nc.tensor.matmul(scores[:, 1, HALF:HALF + 1], wqkv_sb[:, 1], bq_c[:], start=False, stop=True
                             ).then_inc(setup_pe, 1)
            pe.wait_ge(setup_dve, 4)
            nc.tensor.matmul(pv[:, 0:1], w_raw[:], beta_c[:], start=True, stop=False)
            nc.tensor.matmul(pv[:, 0:1], wpT[:], bv_c[:], start=False, stop=True).then_inc(setup_pe, 1)

            pe.wait_ge(setup_dve, 22)
            pe.wait_ge(vareps_ready, 1)
            t_products(0, 0)
            t_products(0, 1)

            def body(b, prev, cur, nxt):
                for s in range(TILES):
                    if cur:
                        score_tile(b, s)
                    if cur and s == 0:
                        pe.wait_ge(tlo_ready, b * 2 + 2)
                        v_products(b, 0)
                    if prev and s == 1:
                        if cur:
                            pe.wait_ge(vlo_ready, b * 2 + 1)
                        spread_inverse(b - 1, 0)
                    if nxt and s == 2:
                        pe.wait_ge(vlo_ready, b * 2 + 1)
                        if prev:
                            pe.wait_ge(r_ready, b * CHUNKS - 1)
                        group_average(b + 1, chan_ready, chan_mv[:, 0:1], mean_psum)
                    if nxt and s == 3:
                        group_average(b + 1, var_ready, var_in[:], var_psum)
                    if cur and s == 4:
                        if nxt:
                            pe.wait_ge(vareps_ready, b + 2)
                        else:
                            pe.wait_ge(r_ready, b * CHUNKS - 1)
                        v_products(b, 1)
                    if prev and s == 5:
                        if cur:
                            pe.wait_ge(vlo_ready, b * 2 + 2)
                        else:
                            pe.wait_ge(r_ready, b * CHUNKS - 1)
                        spread_inverse(b - 1, 1)
                    if nxt and s == 6:
                        pe.wait_ge(vlo_ready, b * 2 + 2)
                        if prev:
                            pe.wait_ge(r_ready, b * CHUNKS)
                    if nxt and s in (6, 7):
                        t_products(b + 1, s - 6)
                    if prev and s < T_LAG:
                        transposes(b - 1, s + TILES - T_LAG)
                    if cur and s >= T_LAG:
                        transposes(b, s - T_LAG)
                    if prev and s < PV_LAG:
                        pv_quarter(b - 1, s + TILES - PV_LAG)
                    if cur and s >= PV_LAG:
                        pv_quarter(b, s - PV_LAG)

            images(pe, body)


_INS = ['x', 'L0_conv_gamma', 'L0_conv_beta', 'L0_conv_w_qkv', 'L0_conv_b_qkv', 'L0_conv_w_proj', 'L0_conv_b_proj']
_OUT = ((4, 128, 32, 32), 'float32')


def kernel(**inputs):
    import numpy as _np
    import concourse.bacc as _bacc
    from concourse import mybir as _mybir
    from concourse.bass_utils import run_bass_kernel_spmd as _run

    nc = _bacc.Bacc("TRN2", target_bir_lowering=False, num_devices=1)
    arrays, args = {}, []
    for name in _INS:
        a = _np.ascontiguousarray(inputs[name])
        arrays[f"in_{name}_dram"] = a
        args.append(nc.dram_tensor(f"in_{name}_dram", a.shape, _mybir.dt.from_np(a.dtype), kind="ExternalInput").ap())
    shape, dtype = _OUT
    out = nc.dram_tensor("out_0_dram", shape, _mybir.dt.from_np(_np.dtype(dtype)), kind="ExternalOutput").ap()
    attention_block(nc, *args, out)
    r = _run(nc, [arrays], core_ids=[0])
    return r.results[0]["out_0_dram"]
```

```python
from contextlib import ExitStack
import math

import concourse.bass as bass
from concourse import mybir

ALU = mybir.AluOpType
ACT = mybir.ActivationFunctionType
F32 = mybir.dt.float32
F16 = mybir.dt.float16
U32 = mybir.dt.uint32
AX_X = mybir.AxisListType.X
RMAX = bass.bass_isa.ReduceOp.max
ds = bass.ds

P = 128
B = 4
N = 1024
GROUP = 4
EPS = 1e-6
HALF = 512
TILES = N // P
CT = HALF // P
CHUNKS = N // HALF
T_LAG = 2
PV_LAG = T_LAG + CT

Z_BOUND = math.sqrt(GROUP * N)
T_MAX = 2.0
C_PER_A = T_MAX * P * Z_BOUND / T_MAX
V_MAX = 4.0
W_LOADS = 4
V_LOADS = 4
TINY = 1e-30
LOG2_P = 10
SUM_MAX = float(N * 2 ** LOG2_P)


def attention_block(nc, x, gamma, beta, w_qkv, b_qkv, w_proj, b_proj, out):
    x_d = x.rearrange("b c h w -> b c (h w)")
    out_d = out.rearrange("b c h w -> b c (h w)")
    col = lambda v: v.rearrange("(c a) -> c a", a=1)
    esc_factor = 1.0 / (T_MAX * math.sqrt(P))

    with ExitStack() as ctx:
        def sb(name, shape, dt=F32):
            return ctx.enter_context(nc.sbuf_tensor(name, shape, dt))

        def pb(name, shape, dt=F32):
            return ctx.enter_context(nc.psum_tensor(name, shape, dt))

        def sem(name):
            return ctx.enter_context(nc.semaphore(name))

        x_sb = sb("x_sb", [P, B * N])
        wqkv_sb = sb("wqkv_sb", [P, 3, P])
        wp_sb = sb("wp_sb", [P, P])
        gamma_c = sb("gamma_c", [P, 1])
        gamma_row = sb("gamma_row", [P, P])
        beta_c = sb("beta_c", [P, 1])
        bq_c = sb("bq_c", [P, 1])
        bv_c = sb("bv_c", [P, 1])
        bp_c = sb("bp_c", [P, 1])
        ident32 = sb("ident32", [P, P])
        ident16 = sb("ident16", [P, P], F16)
        ones16 = sb("ones16", [P, P], F16)
        zero32 = sb("zero32", [P, P])
        group_avg = sb("group_avg", [P, P])
        group_sum = sb("group_sum", [P, P // GROUP])
        minus_half = sb("minus_half", [P, 1])
        wpT = sb("wpT", [P, P])
        a_raw = sb("a_raw", [P, P])
        w_raw = sb("w_raw", [P, P])
        a_mat = sb("a_mat", [P, P])
        w_mat = sb("w_mat", [P, P])
        c_raw = sb("c_raw", [P, 1])
        c_abs = sb("c_abs", [P, 1])
        ct = sb("ct", [P, 1])
        bo = sb("bo", [P, 1])
        wmax = sb("wmax", [P, 3])
        wmax_p = sb("wmax_p", [P, 2])
        wmax_all = sb("wmax_all", [P, 2])
        wmax_safe = sb("wmax_safe", [P, 2])
        winv = sb("winv", [P, 2])
        a_scaled = sb("a_scaled", [P, P])
        w_scaled = sb("w_scaled", [P, P])
        a_hi = sb("a_hi", [P, P], F16)
        a_lo = sb("a_lo", [P, P], F16)
        w_hi = sb("w_hi", [P, P], F16)
        w_lo = sb("w_lo", [P, P], F16)
        esc = sb("esc", [P, 1])
        neg_esc = sb("neg_esc", [P, 1])
        o_scale = sb("o_scale", [P, 1])
        bn = sb("bn", [P, 2, 6])
        bn_seen = sb("bn_seen", [P, 2])
        chan_mv = sb("chan_mv", [P, 2])
        dev = sb("dev", [P, 1])
        var_in = sb("var_in", [P, 1])
        mean_g = sb("mean_g", [P, 1])
        var_eps = sb("var_eps", [P, 1])
        rstd = sb("rstd", [P, 1])
        z32 = sb("z32", [P, N])
        z_hi = sb("z_hi", [P, B * N], F16)
        z_lo = sb("z_lo", [P, B * N], F16)
        t_hi = sb("t_hi", [P, B * N], F16)
        t_lo = sb("t_lo", [P, B * N], F16)
        v_hi = sb("v_hi", [P, B * N], F16)
        v_lo = sb("v_lo", [P, B * N], F16)
        row_max = sb("row_max", [P, 2])
        exp_bias = sb("exp_bias", [P, 2])
        probs = sb("probs", [P, 2, N])
        p_hi = sb("p_hi", [P, 2, N], F16)
        p_lo = sb("p_lo", [P, 2, N], F16)
        row_sum = sb("row_sum", [P, CHUNKS, CT])
        rinv = sb("rinv", [P, CT])
        r_hi = sb("r_hi", [P, CT], F16)
        r_lo = sb("r_lo", [P, CT], F16)
        diag_hi = sb("diag_hi", [P, CT, P], F16)
        diag_lo = sb("diag_lo", [P, CT, P], F16)
        ptT = sb("ptT", [P, CHUNKS, 2, TILES, HALF], F16)
        r_sb = sb("r_sb", [P, HALF])
        attn = sb("attn", [P, HALF])
        out_sb = sb("out_sb", [P, B * N])

        scores = pb("scores", [P, 2, N])
        tr = pb("tr", [P, 2, N], F16)
        pv = pb("pv", [P, HALF])
        misc = pb("misc", [P, HALF])

        x_first = sem("x_first")
        x_rest = sem("x_rest")
        w_loaded = sem("w_loaded")
        v_loaded = sem("v_loaded")
        zeroed = sem("zeroed")
        consts = sem("consts")
        const_dve = sem("const_dve")
        setup_pe = sem("setup_pe")
        setup_dve = sem("setup_dve")
        max_all = sem("max_all")
        bn_done = sem("bn_done")
        chan_ready = sem("chan_ready")
        mean_psum = sem("mean_psum")
        dev_ready = sem("dev_ready")
        var_ready = sem("var_ready")
        var_psum = sem("var_psum")
        mean_ready = sem("mean_ready")
        vareps_ready = sem("vareps_ready")
        rstd_ready = sem("rstd_ready")
        z_ready = sem("z_ready")
        zhi_ready = sem("zhi_ready")
        zlo_ready = sem("zlo_ready")
        t_psum = sem("t_psum")
        thi_ready = sem("thi_ready")
        tlo_ready = sem("tlo_ready")
        v_psum = sem("v_psum")
        vhi_ready = sem("vhi_ready")
        vlo_ready = sem("vlo_ready")
        xb_ready = sem("xb_ready")
        scores_ready = sem("scores_ready")
        max_ready = sem("max_ready")
        bias_ready = sem("bias_ready")
        exp_ready = sem("exp_ready")
        phi_ready = sem("phi_ready")
        plo_ready = sem("plo_ready")
        tr_hi = sem("tr_hi")
        tr_lo = sem("tr_lo")
        ptT_hi = sem("ptT_hi")
        ptT_lo = sem("ptT_lo")
        pv_ready = sem("pv_ready")
        rinv_ready = sem("rinv_ready")
        rhi_ready = sem("rhi_ready")
        rlo_ready = sem("rlo_ready")
        diag_ready = sem("diag_ready")
        r_psum = sem("r_psum")
        r_ready = sem("r_ready")
        attn_ready = sem("attn_ready")
        out_ready = sem("out_ready")
        stored = sem("stored")

        def wait(eng, s, value):
            if not isinstance(value, int) or value > 0:
                eng.wait_ge(s, value)

        def images(eng, body):
            body(0, prev=False, cur=True, nxt=True)
            with eng.Fori(1, B - 1) as b:
                body(b, prev=True, cur=True, nxt=True)
            body(B - 1, prev=True, cur=True, nxt=False)
            body(B, prev=True, cur=False, nxt=False)

        block = ctx.enter_context(nc.Block())

        @block.sync
        def _(sp):
            for half in range(2):
                cols = slice(half * HALF, (half + 1) * HALF)
                sp.dma_start(x_sb[:, cols], x_d[0, :, cols]).then_inc(x_first, 16)
            sp.wait_ge(w_loaded, 16 * W_LOADS)
            for b in range(1, B):
                sp.dma_start(x_sb[:, b * N:(b + 1) * N], x_d[b]).then_inc(x_rest, 16)
            for h in range(B * CHUNKS):
                b, c = divmod(h, CHUNKS)
                sp.wait_ge(out_ready, h + 2)
                sp.dma_start(out_d[b, :, c * HALF:(c + 1) * HALF],
                             out_sb[:, h * HALF:(h + 1) * HALF]).then_inc(stored, 16)
            sp.wait_ge(stored, 16 * B * CHUNKS)

        @block.gpsimd
        def _(pool):
            nc.gpsimd.memset(zero32[:], 0.0).then_inc(zeroed, 1)
            pool.wait_ge(zeroed, 1)
            nc.gpsimd.affine_select(out=ident32[:], in_=zero32[:], compare_op=ALU.not_equal, fill=1.0, base=0,
                                    pattern=[[-1, P]], channel_multiplier=1).then_inc(consts, 1)
            pool.dma_start(beta_c[:], col(beta)).then_inc(v_loaded, 16)
            pool.dma_start(bq_c[:], col(b_qkv[0:P])).then_inc(v_loaded, 16)
            pool.dma_start(bv_c[:], col(b_qkv[2 * P:3 * P])).then_inc(v_loaded, 16)
            pool.dma_start(bp_c[:], col(b_proj)).then_inc(v_loaded, 16)
            def power(b):
                pool.wait_ge(vareps_ready, b + 1)
                nc.gpsimd.tensor_tensor(rstd[:], var_eps[:], minus_half[:], ALU.pow).then_inc(rstd_ready, 1)

            def z_low(b):
                for half in range(2):
                    pool.wait_ge(zhi_ready, b * 2 + half + 1)
                    cols = ds(b * N + half * HALF, HALF)
                    nc.gpsimd.tensor_tensor(z_lo[:, cols], z32[:, half * HALF:(half + 1) * HALF], z_hi[:, cols],
                                            ALU.subtract).then_inc(zlo_ready, 1)

            def p_low(b, s):
                g = b * TILES + s
                pool.wait_ge(exp_ready, g + 1)
                pool.wait_ge(phi_ready, g + 1)
                wait(pool, tr_lo, g - 1)
                nc.gpsimd.tensor_tensor(p_lo[:, s % 2], probs[:, s % 2], p_hi[:, s % 2],
                                        ALU.subtract).then_inc(plo_ready, 1)

            def diagonals(b, c):
                h = b * CHUNKS + c
                wait(pool, r_psum, h)
                pool.wait_ge(rlo_ready, h + 1)
                pool.wait_ge(const_dve, 3)
                eye = ident16[:].unsqueeze(1).broadcast_to([P, CT, P])
                for diag, r in ((diag_hi, r_hi), (diag_lo, r_lo)):
                    nc.gpsimd.tensor_tensor(diag[:], eye, r[:].unsqueeze(2).broadcast_to([P, CT, P]), ALU.mult
                                            ).then_inc(diag_ready, 1)

            def residual(b, c):
                h = b * CHUNKS + c
                pool.wait_ge(attn_ready, h + 2)
                pool.wait_ge(xb_ready, b + 1)
                cols = ds(b * N + c * HALF, HALF)
                nc.gpsimd.tensor_tensor(out_sb[:, cols], attn[:], x_sb[:, cols], ALU.add).then_inc(out_ready, 1)

            power(0)
            pool.wait_ge(setup_dve, 9)
            nc.gpsimd.partition_all_reduce(wmax_all[:], wmax_p[:], P, RMAX).then_inc(max_all, 1)

            def body(b, prev, cur, nxt):
                for s in range(TILES):
                    if prev and s in (2, 6):
                        residual(b - 1, s // CT)
                    if nxt and s == 4:
                        power(b + 1)
                    if nxt and s == 5:
                        z_low(b + 1)
                    if cur:
                        p_low(b, s)
                    if prev and s == 1:
                        diagonals(b - 1, 1)
                    if cur and s == 6:
                        diagonals(b, 0)

            images(pool, body)

        @block.scalar
        def _(act):
            act.dma_start(wqkv_sb[:], w_qkv.rearrange("(t o) c -> o t c", t=3)).then_inc(w_loaded, 16)
            act.dma_start(wp_sb[:], w_proj).then_inc(w_loaded, 16)
            act.dma_start(gamma_row[:], gamma.rearrange("(a c) -> a c", a=1).broadcast_to([P, P])
                          ).then_inc(w_loaded, 16)
            act.dma_start(gamma_c[:], col(gamma)).then_inc(w_loaded, 16)

            def z_high(b):
                for half in range(2):
                    act.wait_ge(z_ready, b * 2 + half + 1)
                    nc.scalar.activation(z_hi[:, ds(b * N + half * HALF, HALF)],
                                         z32[:, half * HALF:(half + 1) * HALF], ACT.Copy).then_inc(zhi_ready, 1)

            def t_high(b, half):
                act.wait_ge(t_psum, b * 2 + half + 1)
                if half == 0:
                    act.wait_ge(setup_dve, 22)
                nc.scalar.activation(t_hi[:, ds(b * N + half * HALF, HALF)], misc[:], ACT.Identity,
                                     bias=ct[:]).then_inc(thi_ready, 1)

            def v_high(b, half):
                act.wait_ge(v_psum, b * 2 + half + 1)
                nc.scalar.activation(v_hi[:, ds(b * N + half * HALF, HALF)], misc[:], ACT.Copy
                                     ).then_inc(vhi_ready, 1)

            def exponentials(b, s):
                g = b * TILES + s
                act.wait_ge(bias_ready, g + 1)
                wait(act, plo_ready, g - 1)
                if s % CT == 0:
                    wait(act, rinv_ready, b * CHUNKS + s // CT - 1)
                nc.scalar.activation(probs[:, s % 2], scores[:, s % 2], ACT.Exp, bias=exp_bias[:, s % 2:s % 2 + 1],
                                     scale=esc[:], accum_out=row_sum[:, s // CT, s % CT:s % CT + 1]
                                     ).then_inc(exp_ready, 1)
                act.wait_ge(exp_ready, g + 1)
                wait(act, tr_hi, g - 1)
                nc.scalar.activation(p_hi[:, s % 2], probs[:, s % 2], ACT.Copy).then_inc(phi_ready, 1)

            def r_copy(b, c):
                h = b * CHUNKS + c
                act.wait_ge(r_psum, h + 1)
                act.wait_ge(attn_ready, h + 1)
                nc.scalar.activation(r_sb[:], misc[:], ACT.Copy).then_inc(r_ready, 1)

            z_high(0)
            t_high(0, 0)

            def body(b, prev, cur, nxt):
                for s in range(TILES):
                    if cur and s == 0:
                        t_high(b, 1)
                    if prev and s in (1, 5):
                        r_copy(b - 1, s // CT)
                    if cur and s in (2, 6):
                        v_high(b, s // CT)
                    if nxt and s == 5:
                        z_high(b + 1)
                    if nxt and s == 7:
                        t_high(b + 1, 0)
                    if cur:
                        exponentials(b, s)
                    if cur and s == 3:
                        nc.scalar.activation(x_sb[:, ds(b * N, N)], x_sb[:, ds(b * N, N)], ACT.Identity,
                                             bias=bo[:]).then_inc(xb_ready, 1)

            images(act, body)

        @block.vector
        def _(dve):
            def channel_stats(b, half):
                if isinstance(b, int) and b == 0:
                    dve.wait_ge(x_first, 32)
                else:
                    dve.wait_ge(x_rest, 16 * (B - 1))
                nc.vector.bn_stats(bn[:, half, :], x_sb[:, ds(b * N + half * HALF, HALF)]).then_inc(bn_done, 1)
                if half == 1:
                    dve.wait_ge(bn_done, b * 2 + 2)
                    nc.vector.tensor_copy(bn_seen[:], bn[:, :, 0])
                    nc.vector.bn_aggr(chan_mv[:], bn[:].rearrange("p a f -> p (a f)")).then_inc(chan_ready, 1)

            nc.vector.memset(minus_half[:], -0.5).then_inc(const_dve, 1)
            nc.vector.memset(ones16[:], 1.0).then_inc(const_dve, 1)
            nc.vector.memset(r_sb[:], 0.0).then_inc(attn_ready, 1)
            nc.vector.memset(attn[:], 0.0).then_inc(out_ready, 1)
            channel_stats(0, 0)
            channel_stats(0, 1)
            dve.wait_ge(consts, 1)
            nc.vector.tensor_copy(ident16[:], ident32[:]).then_inc(const_dve, 1)
            nc.vector.tensor_reduce(group_sum[:], ident32[:].rearrange("p (g j) -> p g j", j=GROUP),
                                    AX_X, ALU.add).then_inc(const_dve, 1)
            dve.wait_ge(const_dve, 4)
            nc.vector.tensor_scalar(group_avg[:].rearrange("p (g j) -> p g j", j=GROUP),
                                    group_sum[:].unsqueeze(2).broadcast_to([P, P // GROUP, GROUP]),
                                    1.0 / GROUP, None, ALU.mult).then_inc(const_dve, 1)

            def group_mean(b):
                dve.wait_ge(mean_psum, b + 1)
                dve.wait_ge(chan_ready, b + 1)
                nc.vector.tensor_tensor(dev[:], chan_mv[:, 0:1], misc[:, 0:1], ALU.subtract).then_inc(dev_ready, 1)
                dve.wait_ge(dev_ready, b + 1)
                nc.vector.scalar_tensor_tensor(out=var_in[:], in0=dev[:], scalar=dev[:], in1=chan_mv[:, 1:2],
                                               op0=ALU.mult, op1=ALU.add).then_inc(var_ready, 1)
                nc.vector.tensor_tensor(mean_g[:], chan_mv[:, 0:1], dev[:], ALU.subtract).then_inc(mean_ready, 1)

            def group_var(b):
                dve.wait_ge(var_psum, b + 1)
                nc.vector.tensor_scalar(var_eps[:], misc[:, 0:1], EPS, None, ALU.add).then_inc(vareps_ready, 1)

            def normalise(b):
                dve.wait_ge(rstd_ready, b + 1)
                dve.wait_ge(mean_ready, b + 1)
                wait(dve, zlo_ready, b * 2)
                for half in range(2):
                    nc.vector.tensor_scalar(z32[:, half * HALF:(half + 1) * HALF],
                                            x_sb[:, ds(b * N + half * HALF, HALF)], mean_g[:], rstd[:],
                                            ALU.subtract, ALU.mult).then_inc(z_ready, 1)

            def z_low_first(half):
                dve.wait_ge(z_ready, half + 1)
                dve.wait_ge(zhi_ready, half + 1)
                cols = slice(half * HALF, (half + 1) * HALF)
                nc.vector.tensor_tensor(z_lo[:, cols], z32[:, cols], z_hi[:, cols], ALU.subtract
                                        ).then_inc(zlo_ready, 1)

            def t_low(b, half):
                dve.wait_ge(thi_ready, b * 2 + half + 1)
                cols = ds(b * N + half * HALF, HALF)
                nc.vector.scalar_tensor_tensor(out=t_lo[:, cols], in0=misc[:], scalar=ct[:], in1=t_hi[:, cols],
                                               op0=ALU.add, op1=ALU.subtract).then_inc(tlo_ready, 1)

            def v_low(b, half):
                dve.wait_ge(vhi_ready, b * 2 + half + 1)
                cols = ds(b * N + half * HALF, HALF)
                nc.vector.tensor_tensor(v_lo[:, cols], misc[:], v_hi[:, cols], ALU.subtract).then_inc(vlo_ready, 1)

            def maxima(b, s):
                g = b * TILES + s
                dve.wait_ge(scores_ready, g + 1)
                nc.vector.tensor_reduce(row_max[:, s % 2:s % 2 + 1], scores[:, s % 2], AX_X, ALU.max
                                        ).then_inc(max_ready, 1)
                dve.wait_ge(max_ready, g + 1)
                wait(dve, exp_ready, g - 1)
                nc.vector.tensor_scalar(exp_bias[:, s % 2:s % 2 + 1], row_max[:, s % 2:s % 2 + 1], neg_esc[:],
                                        LOG2_P * math.log(2.0), ALU.mult, ALU.add).then_inc(bias_ready, 1)

            def take_transposes(b, i):
                g = b * TILES + i
                c, j = divmod(i, CT)
                h = b * CHUNKS + c
                if j == 0:
                    wait(dve, pv_ready, h - CHUNKS + 1)
                for part, (ready, taken) in enumerate(((tr_hi, ptT_hi), (tr_lo, ptT_lo))):
                    dve.wait_ge(ready, g + 1)
                    nc.vector.tensor_copy(
                        ptT[:, c, part, :, j * P:(j + 1) * P].bitcast(U32),
                        tr[:, part].bitcast(U32).rearrange("p (k q) -> p k q", k=TILES)).then_inc(taken, 1)

            def inverse_sums(b, c):
                h = b * CHUNKS + c
                dve.wait_ge(exp_ready, b * TILES + (c + 1) * CT)
                nc.vector.reciprocal(rinv[:], row_sum[:, c]).then_inc(rinv_ready, 1)
                dve.wait_ge(rinv_ready, h + 1)
                wait(dve, diag_ready, 2 * h)
                nc.vector.tensor_scalar(r_hi[:], rinv[:], SUM_MAX, None, ALU.mult).then_inc(rhi_ready, 1)
                dve.wait_ge(rhi_ready, h + 1)
                nc.vector.scalar_tensor_tensor(out=r_lo[:], in0=rinv[:], scalar=SUM_MAX, in1=r_hi[:],
                                               op0=ALU.mult, op1=ALU.subtract).then_inc(rlo_ready, 1)

            def scale_output(b, c):
                h = b * CHUNKS + c
                dve.wait_ge(pv_ready, h + 1)
                dve.wait_ge(r_ready, h + 1)
                dve.wait_ge(out_ready, h + 1)
                nc.vector.scalar_tensor_tensor(out=attn[:], in0=pv[:], scalar=o_scale[:], in1=r_sb[:],
                                               op0=ALU.mult, op1=ALU.mult).then_inc(attn_ready, 1)

            dve.wait_ge(setup_pe, 1)
            nc.vector.tensor_copy(wpT[:], scores[:, 0, 0:P]).then_inc(setup_dve, 1)
            dve.wait_ge(setup_pe, 2)
            nc.vector.tensor_copy(a_raw[:], scores[:, 0, HALF:HALF + P]).then_inc(setup_dve, 1)
            dve.wait_ge(w_loaded, 16 * W_LOADS)
            nc.vector.scalar_tensor_tensor(out=a_mat[:], in0=scores[:, 0, HALF:HALF + P], scalar=gamma_c[:],
                                           in1=gamma_row[:], op0=ALU.mult, op1=ALU.mult).then_inc(setup_dve, 1)
            group_mean(0)
            dve.wait_ge(setup_pe, 3)
            nc.vector.tensor_copy(w_raw[:], scores[:, 1, 0:P]).then_inc(setup_dve, 1)
            nc.vector.tensor_scalar(w_mat[:], scores[:, 1, 0:P], gamma_c[:], None, ALU.mult).then_inc(setup_dve, 1)
            group_var(0)
            dve.wait_ge(setup_dve, 5)
            nc.vector.tensor_reduce(wmax[:, 0:1], a_mat[:], AX_X, ALU.max, apply_absolute_value=True
                                    ).then_inc(setup_dve, 1)
            nc.vector.tensor_reduce(wmax_p[:, 1:2], w_mat[:], AX_X, ALU.max, apply_absolute_value=True
                                    ).then_inc(setup_dve, 1)
            dve.wait_ge(setup_pe, 4)
            nc.vector.tensor_scalar(c_raw[:], scores[:, 1, HALF:HALF + 1], gamma_c[:], None, ALU.mult
                                    ).then_inc(setup_dve, 1)
            dve.wait_ge(setup_dve, 8)
            nc.vector.tensor_reduce(c_abs[:], c_raw[:], AX_X, ALU.max, apply_absolute_value=True
                                    ).then_inc(const_dve, 1)
            dve.wait_ge(const_dve, 6)
            nc.vector.scalar_tensor_tensor(out=wmax_p[:, 0:1], in0=c_abs[:], scalar=1.0 / C_PER_A, in1=wmax[:, 0:1],
                                           op0=ALU.mult, op1=ALU.max).then_inc(setup_dve, 1)
            normalise(0)
            dve.wait_ge(setup_pe, 5)
            dve.wait_ge(v_loaded, 16 * V_LOADS)
            nc.vector.tensor_tensor(bo[:], bp_c[:], pv[:, 0:1], ALU.add).then_inc(setup_dve, 1)
            dve.wait_ge(max_all, 1)
            nc.vector.tensor_scalar(wmax_safe[:], wmax_all[:], TINY, None, ALU.max).then_inc(setup_dve, 1)
            dve.wait_ge(setup_dve, 11)
            nc.vector.reciprocal(winv[:], wmax_safe[:]).then_inc(setup_dve, 1)
            nc.vector.tensor_scalar(esc[:], wmax_safe[:, 0:1], esc_factor, None, ALU.mult).then_inc(setup_dve, 1)
            nc.vector.tensor_scalar(neg_esc[:], wmax_safe[:, 0:1], -esc_factor, None, ALU.mult).then_inc(setup_dve, 1)
            nc.vector.tensor_scalar(o_scale[:], wmax_safe[:, 1:2], 1.0 / (V_MAX * SUM_MAX), None, ALU.mult
                                    ).then_inc(setup_dve, 1)
            dve.wait_ge(setup_dve, 15)
            nc.vector.tensor_scalar(a_scaled[:], a_mat[:], winv[:, 0:1], T_MAX, ALU.mult, ALU.mult
                                    ).then_inc(setup_dve, 1)
            nc.vector.tensor_scalar(w_scaled[:], w_mat[:], winv[:, 1:2], V_MAX, ALU.mult, ALU.mult
                                    ).then_inc(setup_dve, 1)
            nc.vector.tensor_scalar(ct[:], c_raw[:], winv[:, 0:1], T_MAX, ALU.mult, ALU.mult).then_inc(setup_dve, 1)
            dve.wait_ge(setup_dve, 18)
            nc.vector.tensor_copy(a_hi[:], a_scaled[:]).then_inc(setup_dve, 1)
            nc.vector.tensor_copy(w_hi[:], w_scaled[:]).then_inc(setup_dve, 1)
            dve.wait_ge(setup_dve, 20)
            nc.vector.tensor_tensor(a_lo[:], a_scaled[:], a_hi[:], ALU.subtract).then_inc(setup_dve, 1)
            nc.vector.tensor_tensor(w_lo[:], w_scaled[:], w_hi[:], ALU.subtract).then_inc(setup_dve, 1)

            z_low_first(0)
            z_low_first(1)
            t_low(0, 0)

            def body(b, prev, cur, nxt):
                for s in range(TILES):
                    if prev and s in (2, 6):
                        scale_output(b - 1, s // CT)
                    if nxt and s == 3:
                        group_mean(b + 1)
                    if nxt and s == 4:
                        group_var(b + 1)
                    if cur:
                        maxima(b, s)
                    if cur and s == 0:
                        t_low(b, 1)
                    if cur and s in (2, 6):
                        v_low(b, s // CT)
                    if nxt and s == 7:
                        t_low(b + 1, 0)
                    if prev and s < T_LAG:
                        take_transposes(b - 1, s + TILES - T_LAG)
                    if cur and s >= T_LAG:
                        take_transposes(b, s - T_LAG)
                    if prev and s == 1:
                        inverse_sums(b - 1, 1)
                    if cur and s == 5:
                        inverse_sums(b, 0)
                    if nxt and s in (0, 1):
                        channel_stats(b + 1, s)
                    if nxt and s == 4:
                        normalise(b + 1)

            images(dve, body)

        @block.tensor
        def _(pe):
            def group_average(b, source, value, done):
                pe.wait_ge(source, b + 1)
                nc.tensor.matmul(misc[:, 0:1], group_avg[:], value, start=True, stop=True).then_inc(done, 1)

            def t_products(b, half):
                pe.wait_ge(zlo_ready, b * 2 + half + 1)
                if half:
                    pe.wait_ge(tlo_ready, b * 2 + 1)
                cols = ds(b * N + half * HALF, HALF)
                nc.tensor.matmul(misc[:], a_hi[:], z_hi[:, cols], start=True, stop=False)
                nc.tensor.matmul(misc[:], a_hi[:], z_lo[:, cols], start=False, stop=False)
                nc.tensor.matmul(misc[:], a_lo[:], z_hi[:, cols], start=False, stop=True).then_inc(t_psum, 1)

            def v_products(b, half):
                for k in range(CT):
                    cols = ds(b * N + (half * CT + k) * P, P)
                    dst = misc[:, k * P:(k + 1) * P]
                    nc.tensor.matmul(dst, z_hi[:, cols], w_hi[:], start=True, stop=False)
                    nc.tensor.matmul(dst, z_hi[:, cols], w_lo[:], start=False, stop=False)
                    last = nc.tensor.matmul(dst, z_lo[:, cols], w_hi[:], start=False, stop=True)
                last.then_inc(v_psum, 1)

            def score_tile(b, s):
                g = b * TILES + s
                pe.wait_ge(tlo_ready, b * 2 + s // CT + 1)
                wait(pe, exp_ready, g - 1)
                if s == 0:
                    pe.wait_ge(zlo_ready, b * 2 + 2)
                rows = ds(b * N + s * P, P)
                for half in range(2):
                    cols = ds(b * N + half * HALF, HALF)
                    dst = scores[:, s % 2, half * HALF:(half + 1) * HALF]
                    nc.tensor.matmul(dst, t_hi[:, rows], z_hi[:, cols], start=True, stop=False)
                    nc.tensor.matmul(dst, t_hi[:, rows], z_lo[:, cols], start=False, stop=False)
                    last = nc.tensor.matmul(dst, t_lo[:, rows], z_hi[:, cols], start=False, stop=True)
                last.then_inc(scores_ready, 1)

            def transposes(b, i):
                g = b * TILES + i
                for part, (src, ready, taken, done) in enumerate(((p_hi, phi_ready, ptT_hi, tr_hi),
                                                                  (p_lo, plo_ready, ptT_lo, tr_lo))):
                    pe.wait_ge(ready, g + 1)
                    wait(pe, taken, g)
                    for k in range(TILES):
                        last = nc.tensor.transpose(tr[:, part, k * P:(k + 1) * P],
                                                   src[:, i % 2, k * P:(k + 1) * P], ident16[:])
                    last.then_inc(done, 1)

            def pv_quarter(b, r):
                c, quarter = divmod(r, CT)
                h = b * CHUNKS + c
                if quarter == 0:
                    pe.wait_ge(ptT_hi, b * TILES + (c + 1) * CT)
                    pe.wait_ge(ptT_lo, b * TILES + (c + 1) * CT)
                    pe.wait_ge(attn_ready, h + 1)
                if c == 0 and quarter % 2 == 0:
                    pe.wait_ge(vlo_ready, b * 2 + quarter // 2 + 1)
                per = TILES // CT
                for k in range(quarter * per, (quarter + 1) * per):
                    keys = ds(b * N + k * P, P)
                    nc.tensor.matmul(pv[:], v_hi[:, keys], ptT[:, c, 0, k], start=(k == 0), stop=False)
                    nc.tensor.matmul(pv[:], v_hi[:, keys], ptT[:, c, 1, k], start=False, stop=False)
                    last = nc.tensor.matmul(pv[:], v_lo[:, keys], ptT[:, c, 0, k], start=False,
                                            stop=(k == TILES - 1))
                if quarter == CT - 1:
                    last.then_inc(pv_ready, 1)

            def spread_inverse(b, c):
                h = b * CHUNKS + c
                pe.wait_ge(diag_ready, 2 * h + 2)
                nc.tensor.matmul(misc[:], ones16[:], diag_hi[:].rearrange("p a b -> p (a b)"), start=True, stop=False)
                nc.tensor.matmul(misc[:], ones16[:], diag_lo[:].rearrange("p a b -> p (a b)"), start=False, stop=True
                                 ).then_inc(r_psum, 1)

            pe.wait_ge(consts, 1)
            pe.wait_ge(w_loaded, 16 * W_LOADS)
            nc.tensor.transpose(scores[:, 0, 0:P], wp_sb[:], ident32[:]).then_inc(setup_pe, 1)
            nc.tensor.matmul(scores[:, 0, HALF:HALF + P], wqkv_sb[:, 0], wqkv_sb[:, 1], start=True, stop=True
                             ).then_inc(setup_pe, 1)
            pe.wait_ge(const_dve, 5)
            group_average(0, chan_ready, chan_mv[:, 0:1], mean_psum)
            pe.wait_ge(setup_dve, 1)
            nc.tensor.matmul(scores[:, 1, 0:P], wqkv_sb[:, 2], wpT[:], start=True, stop=True).then_inc(setup_pe, 1)
            group_average(0, var_ready, var_in[:], var_psum)
            pe.wait_ge(setup_dve, 2)
            pe.wait_ge(v_loaded, 16 * V_LOADS)
            nc.tensor.matmul(scores[:, 1, HALF:HALF + 1], a_raw[:], beta_c[:], start=True, stop=False)
            nc.tensor.matmul(scores[:, 1, HALF:HALF + 1], wqkv_sb[:, 1], bq_c[:], start=False, stop=True
                             ).then_inc(setup_pe, 1)
            pe.wait_ge(setup_dve, 4)
            nc.tensor.matmul(pv[:, 0:1], w_raw[:], beta_c[:], start=True, stop=False)
            nc.tensor.matmul(pv[:, 0:1], wpT[:], bv_c[:], start=False, stop=True).then_inc(setup_pe, 1)

            pe.wait_ge(setup_dve, 22)
            pe.wait_ge(vareps_ready, 1)
            t_products(0, 0)

            def body(b, prev, cur, nxt):
                for s in range(TILES):
                    if cur:
                        score_tile(b, s)
                    if cur and not prev and s == 0:
                        t_products(0, 1)
                    if prev and s < T_LAG:
                        transposes(b - 1, s + TILES - T_LAG)
                    if cur and s >= T_LAG:
                        transposes(b, s - T_LAG)
                    if cur and s == 1:
                        if prev:
                            pe.wait_ge(r_ready, b * CHUNKS - 1)
                        else:
                            pe.wait_ge(tlo_ready, b * 2 + 2)
                        v_products(b, 0)
                    if cur and s == 5:
                        if prev:
                            pe.wait_ge(r_ready, b * CHUNKS)
                        else:
                            pe.wait_ge(vareps_ready, b + 2)
                        v_products(b, 1)
                    if prev and s < PV_LAG:
                        pv_quarter(b - 1, s + TILES - PV_LAG)
                    if cur and s >= PV_LAG:
                        pv_quarter(b, s - PV_LAG)
                    if prev and s == 0:
                        if cur:
                            pe.wait_ge(tlo_ready, b * 2 + 2)
                        else:
                            pe.wait_ge(vlo_ready, b * 2)
                        spread_inverse(b - 1, 0)
                    if nxt and s == 2:
                        pe.wait_ge(vlo_ready, b * 2 + 1)
                        group_average(b + 1, chan_ready, chan_mv[:, 0:1], mean_psum)
                    if nxt and s == 3:
                        group_average(b + 1, var_ready, var_in[:], var_psum)
                    if prev and s == 4:
                        if nxt:
                            pe.wait_ge(vareps_ready, b + 2)
                        elif cur:
                            pe.wait_ge(vlo_ready, b * 2 + 1)
                        else:
                            pe.wait_ge(r_ready, b * CHUNKS - 1)
                        spread_inverse(b - 1, 1)
                    if nxt and s == 6:
                        pe.wait_ge(vlo_ready, b * 2 + 2)
                        t_products(b + 1, 0)
                    if nxt and s == 7:
                        t_products(b + 1, 1)

            images(pe, body)


_INS = ['x', 'L0_conv_gamma', 'L0_conv_beta', 'L0_conv_w_qkv', 'L0_conv_b_qkv', 'L0_conv_w_proj', 'L0_conv_b_proj']
_OUT = ((4, 128, 32, 32), 'float32')


def kernel(**inputs):
    import numpy as _np
    import concourse.bacc as _bacc
    from concourse import mybir as _mybir
    from concourse.bass_utils import run_bass_kernel_spmd as _run

    nc = _bacc.Bacc("TRN2", target_bir_lowering=False, num_devices=1)
    arrays, args = {}, []
    for name in _INS:
        a = _np.ascontiguousarray(inputs[name])
        arrays[f"in_{name}_dram"] = a
        args.append(nc.dram_tensor(f"in_{name}_dram", a.shape, _mybir.dt.from_np(a.dtype), kind="ExternalInput").ap())
    shape, dtype = _OUT
    out = nc.dram_tensor("out_0_dram", shape, _mybir.dt.from_np(_np.dtype(dtype)), kind="ExternalOutput").ap()
    attention_block(nc, *args, out)
    r = _run(nc, [arrays], core_ids=[0])
    return r.results[0]["out_0_dram"]
```

```python
from contextlib import ExitStack
import math

import concourse.bass as bass
from concourse import mybir

ALU = mybir.AluOpType
ACT = mybir.ActivationFunctionType
F32 = mybir.dt.float32
F16 = mybir.dt.float16
U32 = mybir.dt.uint32
AX_X = mybir.AxisListType.X
RMAX = bass.bass_isa.ReduceOp.max
ds = bass.ds

P = 128
B = 4
N = 1024
GROUP = 4
EPS = 1e-6
HALF = 512
TILES = N // P
CT = HALF // P
CHUNKS = N // HALF
T_LAG = 3
RING = 4
PV_LAG = T_LAG + CT

Z_BOUND = math.sqrt(GROUP * N)
T_MAX = 2.0
C_PER_A = T_MAX * P * Z_BOUND / T_MAX
V_MAX = 4.0
WARM_UP = 8
WARM_GAP = 2
W_LOADS = 3
TINY = 1e-30
LOG2_P = 10
SUM_MAX = float(N * 2 ** LOG2_P)


def attention_block(nc, x, gamma, beta, w_qkv, b_qkv, w_proj, b_proj, out):
    x_d = x.rearrange("b c h w -> b c (h w)")
    out_d = out.rearrange("b c h w -> b c (h w)")
    col = lambda v: v.rearrange("(c a) -> c a", a=1)

    with ExitStack() as ctx:
        def sb(name, shape, dt=F32):
            return ctx.enter_context(nc.sbuf_tensor(name, shape, dt))

        def pb(name, shape, dt=F32):
            return ctx.enter_context(nc.psum_tensor(name, shape, dt))

        def sem(name):
            return ctx.enter_context(nc.semaphore(name))

        x_sb = sb("x_sb", [P, B * N])
        wqkv_sb = sb("wqkv_sb", [P, 3, P])
        wp_sb = sb("wp_sb", [P, P])
        gamma_c = sb("gamma_c", [P, 1])
        gamma_row = sb("gamma_row", [P, P])
        beta_c = sb("beta_c", [P, 1])
        bq_c = sb("bq_c", [P, 1])
        bv_c = sb("bv_c", [P, 1])
        bp_c = sb("bp_c", [P, 1])
        ident32 = sb("ident32", [P, P])
        ident16 = sb("ident16", [P, P], F16)
        ones16 = sb("ones16", [P, P], F16)
        warm = sb("warm", [P, HALF], F16)
        zero32 = sb("zero32", [P, P])
        group_avg = sb("group_avg", [P, P])
        group_sum = sb("group_sum", [P, P // GROUP])
        minus_half = sb("minus_half", [P, 1])
        wpT = sb("wpT", [P, P])
        a_raw = sb("a_raw", [P, P])
        w_raw = sb("w_raw", [P, P])
        a_mat = sb("a_mat", [P, P])
        w_mat = sb("w_mat", [P, P])
        c_raw = sb("c_raw", [P, 1])
        c_abs = sb("c_abs", [P, 1])
        ct = sb("ct", [P, 1])
        bo = sb("bo", [P, 1])
        a_rowmax = sb("a_rowmax", [P, 1])
        a_max = sb("a_max", [P, 4])
        w_max = sb("w_max", [P, 4])
        a_inv = sb("a_inv", [P, 1])
        w_inv = sb("w_inv", [P, 1])
        a_hi = sb("a_hi", [P, P], F16)
        a_lo = sb("a_lo", [P, P], F16)
        w_hi = sb("w_hi", [P, P], F16)
        w_lo = sb("w_lo", [P, P], F16)
        esc = sb("esc", [P, 1])
        neg_esc = sb("neg_esc", [P, 1])
        o_scale = sb("o_scale", [P, 1])
        bn = sb("bn", [P, 2, 6])
        bn_seen = sb("bn_seen", [P, 2])
        chan_mv = sb("chan_mv", [P, 2])
        dev = sb("dev", [P, 1])
        var_in = sb("var_in", [P, 1])
        mean_g = sb("mean_g", [P, 1])
        var_eps = sb("var_eps", [P, 1])
        rstd = sb("rstd", [P, 1])
        z32 = sb("z32", [P, N])
        z_hi = sb("z_hi", [P, B * N], F16)
        z_lo = sb("z_lo", [P, B * N], F16)
        t_hi = sb("t_hi", [P, B * N], F16)
        t_lo = sb("t_lo", [P, B * N], F16)
        v_hi = sb("v_hi", [P, B * N], F16)
        v_lo = sb("v_lo", [P, B * N], F16)
        row_max = sb("row_max", [P, 2])
        exp_bias = sb("exp_bias", [P, 2])
        probs = sb("probs", [P, RING, N])
        p_hi = sb("p_hi", [P, RING, N], F16)
        p_lo = sb("p_lo", [P, RING, N], F16)
        row_sum = sb("row_sum", [P, CHUNKS, CT])
        rinv = sb("rinv", [P, CT])
        r_hi = sb("r_hi", [P, CT], F16)
        r_lo = sb("r_lo", [P, CT], F16)
        diag_hi = sb("diag_hi", [P, CT, P], F16)
        diag_lo = sb("diag_lo", [P, CT, P], F16)
        ptT = sb("ptT", [P, CHUNKS, 2, TILES, HALF], F16)
        r_sb = sb("r_sb", [P, HALF])
        attn = sb("attn", [P, HALF])
        out_sb = sb("out_sb", [P, B * N])

        scores = pb("scores", [P, 2, N])
        tr = pb("tr", [P, 2, N], F16)
        pv = pb("pv", [P, HALF])
        misc = pb("misc", [P, HALF])

        x_first = [sem("x_first0"), sem("x_first1")]
        x_rest = sem("x_rest")
        wqkv_loaded = sem("wqkv_loaded")
        w_loaded = sem("w_loaded")
        c_loaded = sem("c_loaded")
        o_loaded = sem("o_loaded")
        zeroed = sem("zeroed")
        consts = sem("consts")
        const_dve = sem("const_dve")
        const_warm = sem("const_warm")
        a_psum = sem("a_psum")
        c_psum = sem("c_psum")
        wpT_psum = sem("wpT_psum")
        w_psum = sem("w_psum")
        bo_psum = sem("bo_psum")
        araw_ready = sem("araw_ready")
        amat_ready = sem("amat_ready")
        amax_row = sem("amax_row")
        craw_ready = sem("craw_ready")
        cabs_ready = sem("cabs_ready")
        amax_ready = sem("amax_ready")
        amax_all = sem("amax_all")
        amax_safe = sem("amax_safe")
        ainv_ready = sem("ainv_ready")
        ahi_ready = sem("ahi_ready")
        a_ready = sem("a_ready")
        wpT_ready = sem("wpT_ready")
        wraw_ready = sem("wraw_ready")
        wmat_ready = sem("wmat_ready")
        wmax_ready = sem("wmax_ready")
        wmax_all = sem("wmax_all")
        wmax_safe = sem("wmax_safe")
        winv_ready = sem("winv_ready")
        whi_ready = sem("whi_ready")
        w_ready = sem("w_ready")
        bn_done = sem("bn_done")
        chan_ready = sem("chan_ready")
        mean_psum = sem("mean_psum")
        dev_ready = sem("dev_ready")
        var_ready = sem("var_ready")
        var_psum = sem("var_psum")
        mean_ready = sem("mean_ready")
        vareps_ready = sem("vareps_ready")
        rstd_ready = sem("rstd_ready")
        z_ready = sem("z_ready")
        zhi_ready = sem("zhi_ready")
        zlo_ready = sem("zlo_ready")
        t_psum = sem("t_psum")
        thi_ready = sem("thi_ready")
        tlo_ready = sem("tlo_ready")
        v_psum = sem("v_psum")
        vhi_ready = sem("vhi_ready")
        vlo_ready = sem("vlo_ready")
        xb_ready = sem("xb_ready")
        scores_ready = sem("scores_ready")
        max_ready = sem("max_ready")
        bias_ready = sem("bias_ready")
        exp_ready = sem("exp_ready")
        phi_ready = sem("phi_ready")
        plo_ready = sem("plo_ready")
        tr_hi = sem("tr_hi")
        tr_lo = sem("tr_lo")
        ptT_hi_even = sem("ptT_hi_even")
        ptT_hi_odd = sem("ptT_hi_odd")
        ptT_lo = sem("ptT_lo")
        pv_ready = sem("pv_ready")
        rinv_ready = sem("rinv_ready")
        rhi_ready = sem("rhi_ready")
        rlo_ready = sem("rlo_ready")
        diag_ready = sem("diag_ready")
        r_psum = sem("r_psum")
        r_ready = sem("r_ready")
        attn_ready = sem("attn_ready")
        out_ready = sem("out_ready")
        stored = sem("stored")

        def wait(eng, s, value):
            if not isinstance(value, int) or value > 0:
                eng.wait_ge(s, value)

        def images(eng, body):
            body(0, prev=False, cur=True, nxt=True)
            with eng.Fori(1, B - 1) as b:
                body(b, prev=True, cur=True, nxt=True)
            body(B - 1, prev=True, cur=True, nxt=False)
            body(B, prev=True, cur=False, nxt=False)

        block = ctx.enter_context(nc.Block())

        @block.sync
        def _(sp):
            for half in range(2):
                cols = slice(half * HALF, (half + 1) * HALF)
                sp.dma_start(x_sb[:, cols], x_d[0, :, cols]).then_inc(x_first[half], 16)
            sp.wait_ge(w_loaded, 16 * W_LOADS)
            for b in range(1, B):
                sp.dma_start(x_sb[:, b * N:(b + 1) * N], x_d[b]).then_inc(x_rest, 16)
            for h in range(B * CHUNKS - 1):
                b, c = divmod(h, CHUNKS)
                sp.wait_ge(out_ready, h + 2)
                sp.dma_start(out_d[b, :, c * HALF:(c + 1) * HALF],
                             out_sb[:, h * HALF:(h + 1) * HALF]).then_inc(stored, 16)
            for q in range(2):
                sp.wait_ge(out_ready, B * CHUNKS + 1 + q)
                start = N - HALF + q * HALF // 2
                sp.dma_start(out_d[B - 1, :, start:start + HALF // 2],
                             out_sb[:, (B - 1) * N + start:(B - 1) * N + start + HALF // 2]).then_inc(stored, 16)
            sp.wait_ge(stored, 16 * (B * CHUNKS + 1))

        @block.gpsimd
        def _(pool):
            nc.gpsimd.memset(zero32[:], 0.0).then_inc(zeroed, 1)
            pool.wait_ge(zeroed, 1)
            nc.gpsimd.affine_select(out=ident32[:], in_=zero32[:], compare_op=ALU.not_equal, fill=1.0, base=0,
                                    pattern=[[-1, P]], channel_multiplier=1).then_inc(consts, 1)
            pool.dma_start(beta_c[:], col(beta)).then_inc(c_loaded, 16)
            pool.dma_start(bq_c[:], col(b_qkv[0:P])).then_inc(c_loaded, 16)
            pool.dma_start(bv_c[:], col(b_qkv[2 * P:3 * P])).then_inc(o_loaded, 16)
            pool.dma_start(bp_c[:], col(b_proj)).then_inc(o_loaded, 16)
            def power(b):
                pool.wait_ge(vareps_ready, b + 1)
                nc.gpsimd.tensor_tensor(rstd[:], var_eps[:], minus_half[:], ALU.pow).then_inc(rstd_ready, 1)

            def z_low(b):
                for half in range(2):
                    pool.wait_ge(zhi_ready, b * 2 + half + 1)
                    cols = ds(b * N + half * HALF, HALF)
                    nc.gpsimd.tensor_tensor(z_lo[:, cols], z32[:, half * HALF:(half + 1) * HALF], z_hi[:, cols],
                                            ALU.subtract).then_inc(zlo_ready, 1)

            def p_low(b, s):
                g = b * TILES + s
                pool.wait_ge(exp_ready, g + 1)
                pool.wait_ge(phi_ready, g + 1)
                wait(pool, tr_lo, g - RING + 1)
                nc.gpsimd.tensor_tensor(p_lo[:, s % RING], probs[:, s % RING], p_hi[:, s % RING],
                                        ALU.subtract).then_inc(plo_ready, 1)

            def diagonals(b, c):
                h = b * CHUNKS + c
                wait(pool, r_psum, h)
                pool.wait_ge(rlo_ready, h + 1)
                eye = ident16[:].unsqueeze(1).broadcast_to([P, CT, P])
                for diag, r in ((diag_hi, r_hi), (diag_lo, r_lo)):
                    nc.gpsimd.tensor_tensor(diag[:], eye, r[:].unsqueeze(2).broadcast_to([P, CT, P]), ALU.mult
                                            ).then_inc(diag_ready, 1)

            def residual(b, c):
                h = b * CHUNKS + c
                pool.wait_ge(attn_ready, h + 2)
                pool.wait_ge(xb_ready, b + 1)
                cols = ds(b * N + c * HALF, HALF)
                nc.gpsimd.tensor_tensor(out_sb[:, cols], attn[:], x_sb[:, cols], ALU.add).then_inc(out_ready, 1)

            pool.wait_ge(const_dve, 3)
            power(0)
            pool.wait_ge(amax_ready, 1)
            nc.gpsimd.partition_all_reduce(a_max[:, 1:2], a_max[:, 0:1], P, RMAX).then_inc(amax_all, 1)
            pool.wait_ge(wmax_ready, 1)
            nc.gpsimd.partition_all_reduce(w_max[:, 1:2], w_max[:, 0:1], P, RMAX).then_inc(wmax_all, 1)

            def body(b, prev, cur, nxt):
                for s in range(TILES):
                    if prev and (cur or s < CT) and s in (3, 7):
                        residual(b - 1, s // CT)
                    if nxt and s == (4 if prev else 3):
                        power(b + 1)
                    if nxt and s == 5:
                        z_low(b + 1)
                    if cur:
                        p_low(b, s)
                    if prev and s == 2:
                        diagonals(b - 1, 1)
                    if cur and s == 6:
                        diagonals(b, 0)

            images(pool, body)

        @block.scalar
        def _(act):
            act.dma_start(wqkv_sb[:], w_qkv.rearrange("(t o) c -> o t c", t=3)).then_inc(wqkv_loaded, 16)
            act.dma_start(wp_sb[:], w_proj).then_inc(w_loaded, 16)
            act.dma_start(gamma_row[:], gamma.rearrange("(a c) -> a c", a=1).broadcast_to([P, P])
                          ).then_inc(w_loaded, 16)
            act.dma_start(gamma_c[:], col(gamma)).then_inc(w_loaded, 16)

            def z_high(b):
                for half in range(2):
                    act.wait_ge(z_ready, b * 2 + half + 1)
                    nc.scalar.activation(z_hi[:, ds(b * N + half * HALF, HALF)],
                                         z32[:, half * HALF:(half + 1) * HALF], ACT.Copy).then_inc(zhi_ready, 1)

            def t_high(b, half):
                act.wait_ge(t_psum, b * 2 + half + 1)
                if half == 0:
                    act.wait_ge(a_ready, 5)
                nc.scalar.activation(t_hi[:, ds(b * N + half * HALF, HALF)], misc[:], ACT.Identity,
                                     bias=ct[:]).then_inc(thi_ready, 1)

            def v_high(b, half):
                act.wait_ge(v_psum, b * 2 + half + 1)
                nc.scalar.activation(v_hi[:, ds(b * N + half * HALF, HALF)], misc[:], ACT.Copy
                                     ).then_inc(vhi_ready, 1)

            def exponentials(b, s):
                g = b * TILES + s
                act.wait_ge(bias_ready, g + 1)
                wait(act, plo_ready, g - RING + 1)
                if s % CT == 0:
                    wait(act, rinv_ready, b * CHUNKS + s // CT - 1)
                nc.scalar.activation(probs[:, s % RING], scores[:, s % 2], ACT.Exp, bias=exp_bias[:, s % 2:s % 2 + 1],
                                     scale=esc[:], accum_out=row_sum[:, s // CT, s % CT:s % CT + 1]
                                     ).then_inc(exp_ready, 1)

            def p_high(b, s):
                g = b * TILES + s
                act.wait_ge(exp_ready, g + 1)
                wait(act, tr_hi, g - RING + 1)
                nc.scalar.activation(p_hi[:, s % RING], probs[:, s % RING], ACT.Copy).then_inc(phi_ready, 1)

            def take_high(b, i):
                c, j = divmod(i, CT)
                if j == 0:
                    wait(act, pv_ready, (b - 1) * CHUNKS + c + 1)
                act.wait_ge(tr_hi, b * TILES + i + 1)
                nc.scalar.activation(ptT[:, c, 0, :, j * P:(j + 1) * P],
                                     tr[:, 0].rearrange("p (k q) -> p k q", k=TILES), ACT.Copy
                                     ).then_inc(ptT_hi_even, 1)

            def r_copy(b, c):
                h = b * CHUNKS + c
                act.wait_ge(r_psum, h + 1)
                act.wait_ge(attn_ready, h + 1)
                nc.scalar.activation(r_sb[:], misc[:], ACT.Copy).then_inc(r_ready, 1)

            act.wait_ge(amat_ready, 1)
            nc.scalar.activation(a_raw[:], scores[:, 0, 0:P], ACT.Copy).then_inc(araw_ready, 1)
            act.wait_ge(wpT_psum, 1)
            nc.scalar.activation(wpT[:], scores[:, 1, 0:P], ACT.Copy).then_inc(wpT_ready, 1)
            z_high(0)
            t_high(0, 0)
            act.wait_ge(wmat_ready, 1)
            nc.scalar.activation(w_raw[:], scores[:, 1, HALF:HALF + P], ACT.Copy).then_inc(wraw_ready, 1)

            def body(b, prev, cur, nxt):
                for s in range(TILES):
                    if cur and s == 0:
                        t_high(b, 1)
                    if prev and s in (1, 5):
                        r_copy(b - 1, s // CT)
                    if nxt and s == 5:
                        z_high(b + 1)
                    if nxt and s == 7:
                        t_high(b + 1, 0)
                    if prev and s == 1:
                        take_high(b - 1, s + TILES - T_LAG)
                    if cur and s >= T_LAG and (s - T_LAG) % 2 == 0:
                        take_high(b, s - T_LAG)
                    if cur:
                        exponentials(b, s)
                    if cur and s in (1, 5):
                        v_high(b, s // CT)
                    if cur:
                        p_high(b, s)
                    if cur and s == 3:
                        if not prev:
                            act.wait_ge(w_ready, 3)
                        nc.scalar.activation(x_sb[:, ds(b * N, N)], x_sb[:, ds(b * N, N)], ACT.Identity,
                                             bias=bo[:]).then_inc(xb_ready, 1)

            images(act, body)

        @block.vector
        def _(dve):
            def channel_stats(b, half):
                if isinstance(b, int) and b == 0:
                    dve.wait_ge(x_first[half], 16)
                else:
                    dve.wait_ge(x_rest, 16 * (B - 1))
                nc.vector.bn_stats(bn[:, half, :], x_sb[:, ds(b * N + half * HALF, HALF)]).then_inc(bn_done, 1)
                if half == 1:
                    dve.wait_ge(bn_done, b * 2 + 2)
                    nc.vector.tensor_copy(bn_seen[:], bn[:, :, 0])
                    nc.vector.bn_aggr(chan_mv[:], bn[:].rearrange("p a f -> p (a f)")).then_inc(chan_ready, 1)

            nc.vector.memset(minus_half[:], -0.5).then_inc(const_dve, 1)
            nc.vector.memset(ones16[:], 1.0).then_inc(const_dve, 1)
            nc.vector.memset(warm[:], 0.0).then_inc(const_warm, 1)
            nc.vector.memset(r_sb[:], 0.0).then_inc(attn_ready, 1)
            nc.vector.memset(attn[:], 0.0).then_inc(out_ready, 1)
            dve.wait_ge(consts, 1)
            nc.vector.tensor_copy(ident16[:], ident32[:]).then_inc(const_dve, 1)
            nc.vector.tensor_reduce(group_sum[:], ident32[:].rearrange("p (g j) -> p g j", j=GROUP),
                                    AX_X, ALU.add).then_inc(const_dve, 1)
            dve.wait_ge(const_dve, 4)
            nc.vector.tensor_scalar(group_avg[:].rearrange("p (g j) -> p g j", j=GROUP),
                                    group_sum[:].unsqueeze(2).broadcast_to([P, P // GROUP, GROUP]),
                                    1.0 / GROUP, None, ALU.mult).then_inc(const_dve, 1)

            def group_mean(b):
                dve.wait_ge(mean_psum, b + 1)
                dve.wait_ge(chan_ready, b + 1)
                nc.vector.tensor_tensor(dev[:], chan_mv[:, 0:1], misc[:, 0:1], ALU.subtract).then_inc(dev_ready, 1)
                dve.wait_ge(dev_ready, b + 1)
                nc.vector.scalar_tensor_tensor(out=var_in[:], in0=dev[:], scalar=dev[:], in1=chan_mv[:, 1:2],
                                               op0=ALU.mult, op1=ALU.add).then_inc(var_ready, 1)
                nc.vector.tensor_tensor(mean_g[:], chan_mv[:, 0:1], dev[:], ALU.subtract).then_inc(mean_ready, 1)

            def group_var(b):
                dve.wait_ge(var_psum, b + 1)
                nc.vector.tensor_scalar(var_eps[:], misc[:, 0:1], EPS, None, ALU.add).then_inc(vareps_ready, 1)

            def normalise(b):
                dve.wait_ge(rstd_ready, b + 1)
                dve.wait_ge(mean_ready, b + 1)
                wait(dve, zlo_ready, b * 2)
                for half in range(2):
                    nc.vector.tensor_scalar(z32[:, half * HALF:(half + 1) * HALF],
                                            x_sb[:, ds(b * N + half * HALF, HALF)], mean_g[:], rstd[:],
                                            ALU.subtract, ALU.mult).then_inc(z_ready, 1)

            def z_low_first(half):
                dve.wait_ge(z_ready, half + 1)
                dve.wait_ge(zhi_ready, half + 1)
                cols = slice(half * HALF, (half + 1) * HALF)
                nc.vector.tensor_tensor(z_lo[:, cols], z32[:, cols], z_hi[:, cols], ALU.subtract
                                        ).then_inc(zlo_ready, 1)

            def t_low(b, half):
                dve.wait_ge(thi_ready, b * 2 + half + 1)
                cols = ds(b * N + half * HALF, HALF)
                nc.vector.scalar_tensor_tensor(out=t_lo[:, cols], in0=misc[:], scalar=ct[:], in1=t_hi[:, cols],
                                               op0=ALU.add, op1=ALU.subtract).then_inc(tlo_ready, 1)

            def v_low(b, half):
                dve.wait_ge(vhi_ready, b * 2 + half + 1)
                cols = ds(b * N + half * HALF, HALF)
                nc.vector.tensor_tensor(v_lo[:, cols], misc[:], v_hi[:, cols], ALU.subtract).then_inc(vlo_ready, 1)

            def maxima(b, s):
                g = b * TILES + s
                dve.wait_ge(scores_ready, g + 1)
                nc.vector.tensor_reduce(row_max[:, s % 2:s % 2 + 1], scores[:, s % 2], AX_X, ALU.max
                                        ).then_inc(max_ready, 1)
                dve.wait_ge(max_ready, g + 1)
                wait(dve, exp_ready, g - 1)
                nc.vector.tensor_scalar(exp_bias[:, s % 2:s % 2 + 1], row_max[:, s % 2:s % 2 + 1], neg_esc[:],
                                        LOG2_P * math.log(2.0), ALU.mult, ALU.add).then_inc(bias_ready, 1)

            def take_transposes(b, i):
                g = b * TILES + i
                c, j = divmod(i, CT)
                h = b * CHUNKS + c
                if j == 0:
                    wait(dve, pv_ready, h - CHUNKS + 1)
                for part, (ready, taken) in enumerate(((tr_hi, ptT_hi_odd), (tr_lo, ptT_lo))):
                    if part == 0 and i % 2 == 0:
                        continue
                    dve.wait_ge(ready, g + 1)
                    nc.vector.tensor_copy(
                        ptT[:, c, part, :, j * P:(j + 1) * P].bitcast(U32),
                        tr[:, part].bitcast(U32).rearrange("p (k q) -> p k q", k=TILES)).then_inc(taken, 1)

            def inverse_sums(b, c):
                h = b * CHUNKS + c
                dve.wait_ge(exp_ready, b * TILES + (c + 1) * CT)
                nc.vector.reciprocal(rinv[:], row_sum[:, c]).then_inc(rinv_ready, 1)
                dve.wait_ge(rinv_ready, h + 1)
                wait(dve, diag_ready, h * 2)
                nc.vector.tensor_scalar(r_hi[:], rinv[:], SUM_MAX, None, ALU.mult).then_inc(rhi_ready, 1)
                dve.wait_ge(rhi_ready, h + 1)
                nc.vector.scalar_tensor_tensor(out=r_lo[:], in0=rinv[:], scalar=SUM_MAX, in1=r_hi[:],
                                               op0=ALU.mult, op1=ALU.subtract).then_inc(rlo_ready, 1)

            def last_chunk():
                dve.wait_ge(r_ready, B * CHUNKS)
                dve.wait_ge(xb_ready, B)
                dve.wait_ge(out_ready, B * CHUNKS)
                for q in range(2):
                    cols = slice(q * HALF // 2, (q + 1) * HALF // 2)
                    start = B * N - HALF + q * HALF // 2
                    dve.wait_ge(pv_ready, B * CHUNKS + q)
                    nc.vector.scalar_tensor_tensor(out=attn[:, cols], in0=scores[:, q, 0:HALF // 2],
                                                   scalar=o_scale[:], in1=r_sb[:, cols], op0=ALU.mult, op1=ALU.mult
                                                   ).then_inc(attn_ready, 1)
                    dve.wait_ge(attn_ready, B * CHUNKS + 1 + q)
                    nc.vector.tensor_tensor(out_sb[:, start:start + HALF // 2], attn[:, cols],
                                            x_sb[:, start:start + HALF // 2], ALU.add).then_inc(out_ready, 1)

            def scale_output(b, c):
                h = b * CHUNKS + c
                dve.wait_ge(pv_ready, h + 1)
                dve.wait_ge(r_ready, h + 1)
                dve.wait_ge(out_ready, h + 1)
                nc.vector.scalar_tensor_tensor(out=attn[:], in0=pv[:], scalar=o_scale[:], in1=r_sb[:],
                                               op0=ALU.mult, op1=ALU.mult).then_inc(attn_ready, 1)

            channel_stats(0, 0)
            channel_stats(0, 1)

            dve.wait_ge(w_loaded, 16 * W_LOADS)
            dve.wait_ge(a_psum, 1)
            nc.vector.scalar_tensor_tensor(out=a_mat[:], in0=scores[:, 0, 0:P], scalar=gamma_c[:],
                                           in1=gamma_row[:], op0=ALU.mult, op1=ALU.mult).then_inc(amat_ready, 1)
            dve.wait_ge(amat_ready, 1)
            nc.vector.tensor_reduce(a_rowmax[:], a_mat[:], AX_X, ALU.max, apply_absolute_value=True
                                    ).then_inc(amax_row, 1)
            group_mean(0)
            dve.wait_ge(c_psum, 1)
            nc.vector.tensor_scalar(c_raw[:], scores[:, 0, HALF:HALF + 1], gamma_c[:], None, ALU.mult
                                    ).then_inc(craw_ready, 1)
            dve.wait_ge(craw_ready, 1)
            nc.vector.tensor_reduce(c_abs[:], c_raw[:], AX_X, ALU.max, apply_absolute_value=True
                                    ).then_inc(cabs_ready, 1)
            dve.wait_ge(cabs_ready, 1)
            dve.wait_ge(amax_row, 1)
            nc.vector.scalar_tensor_tensor(out=a_max[:, 0:1], in0=c_abs[:], scalar=1.0 / C_PER_A, in1=a_rowmax[:],
                                           op0=ALU.mult, op1=ALU.max).then_inc(amax_ready, 1)
            group_var(0)
            normalise(0)
            dve.wait_ge(amax_all, 1)
            nc.vector.tensor_scalar(a_max[:, 2:3], a_max[:, 1:2], 1.0 / T_MAX, TINY, ALU.mult, ALU.max
                                    ).then_inc(amax_safe, 1)
            dve.wait_ge(amax_safe, 1)
            nc.vector.reciprocal(a_inv[:], a_max[:, 2:3]).then_inc(ainv_ready, 1)
            nc.vector.tensor_scalar(esc[:], a_max[:, 2:3], 1.0 / math.sqrt(P), None, ALU.mult).then_inc(a_ready, 1)
            nc.vector.tensor_scalar(neg_esc[:], a_max[:, 2:3], -1.0 / math.sqrt(P), None, ALU.mult
                                    ).then_inc(a_ready, 1)
            dve.wait_ge(ainv_ready, 1)
            nc.vector.tensor_scalar(a_hi[:], a_mat[:], a_inv[:], None, ALU.mult).then_inc(ahi_ready, 1)
            nc.vector.tensor_scalar(ct[:], c_raw[:], a_inv[:], None, ALU.mult).then_inc(a_ready, 1)
            z_low_first(0)
            dve.wait_ge(ahi_ready, 1)
            nc.vector.scalar_tensor_tensor(out=a_lo[:], in0=a_mat[:], scalar=a_inv[:], in1=a_hi[:],
                                           op0=ALU.mult, op1=ALU.subtract).then_inc(a_ready, 2)
            z_low_first(1)
            dve.wait_ge(w_psum, 1)
            nc.vector.tensor_scalar(w_mat[:], scores[:, 1, HALF:HALF + P], gamma_c[:], None, ALU.mult
                                    ).then_inc(wmat_ready, 1)
            dve.wait_ge(wmat_ready, 1)
            nc.vector.tensor_reduce(w_max[:, 0:1], w_mat[:], AX_X, ALU.max, apply_absolute_value=True
                                    ).then_inc(wmax_ready, 1)
            t_low(0, 0)
            dve.wait_ge(wmax_all, 1)
            nc.vector.tensor_scalar(w_max[:, 2:3], w_max[:, 1:2], 1.0 / V_MAX, TINY, ALU.mult, ALU.max
                                    ).then_inc(wmax_safe, 1)
            dve.wait_ge(wmax_safe, 1)
            nc.vector.reciprocal(w_inv[:], w_max[:, 2:3]).then_inc(winv_ready, 1)
            nc.vector.tensor_scalar(o_scale[:], w_max[:, 2:3], 1.0 / SUM_MAX, None, ALU.mult).then_inc(w_ready, 1)
            dve.wait_ge(winv_ready, 1)
            nc.vector.tensor_scalar(w_hi[:], w_mat[:], w_inv[:], None, ALU.mult).then_inc(whi_ready, 1)
            dve.wait_ge(whi_ready, 1)
            nc.vector.scalar_tensor_tensor(out=w_lo[:], in0=w_mat[:], scalar=w_inv[:], in1=w_hi[:],
                                           op0=ALU.mult, op1=ALU.subtract).then_inc(w_ready, 1)
            dve.wait_ge(bo_psum, 1)
            dve.wait_ge(o_loaded, 32)
            nc.vector.tensor_tensor(bo[:], bp_c[:], pv[:, 0:1], ALU.add).then_inc(w_ready, 1)

            def body(b, prev, cur, nxt):
                for s in range(TILES):
                    if prev and (cur or s < CT) and s in (3, 7):
                        scale_output(b - 1, s // CT)
                    if not cur and s == 7:
                        last_chunk()
                    if prev and nxt and s == 3:
                        group_mean(b + 1)
                    if prev and nxt and s == 4:
                        group_var(b + 1)
                    if prev and nxt and s == 7:
                        t_low(b + 1, 0)
                    if cur:
                        maxima(b, s)
                    if not prev and s == 3:
                        group_mean(b + 1)
                    if not prev and s == 4:
                        group_var(b + 1)
                    if cur and s == 0:
                        t_low(b, 1)
                    if cur and s in (2, 6):
                        v_low(b, s // CT)
                    if not prev and s == 7:
                        t_low(b + 1, 0)
                    if prev and s < T_LAG:
                        take_transposes(b - 1, s + TILES - T_LAG)
                    if cur and s >= T_LAG:
                        take_transposes(b, s - T_LAG)
                    if prev and s == 1:
                        inverse_sums(b - 1, 1)
                    if cur and s == 5:
                        inverse_sums(b, 0)
                    if nxt and s in (0, 1):
                        channel_stats(b + 1, s)
                    if nxt and s == 4:
                        normalise(b + 1)

            images(dve, body)

        @block.tensor
        def _(pe):
            def group_average(b, source, value, done):
                pe.wait_ge(source, b + 1)
                nc.tensor.matmul(misc[:, 0:1], group_avg[:], value, start=True, stop=True).then_inc(done, 1)

            def t_products(b, half):
                pe.wait_ge(zlo_ready, b * 2 + half + 1)
                if half:
                    pe.wait_ge(tlo_ready, b * 2 + 1)
                cols = ds(b * N + half * HALF, HALF)
                nc.tensor.matmul(misc[:], a_hi[:], z_hi[:, cols], start=True, stop=False)
                nc.tensor.matmul(misc[:], a_hi[:], z_lo[:, cols], start=False, stop=False)
                nc.tensor.matmul(misc[:], a_lo[:], z_hi[:, cols], start=False, stop=True).then_inc(t_psum, 1)

            def v_products(b, half):
                for k in range(CT):
                    cols = ds(b * N + (half * CT + k) * P, P)
                    dst = misc[:, k * P:(k + 1) * P]
                    nc.tensor.matmul(dst, z_hi[:, cols], w_hi[:], start=True, stop=False)
                    nc.tensor.matmul(dst, z_hi[:, cols], w_lo[:], start=False, stop=False)
                    last = nc.tensor.matmul(dst, z_lo[:, cols], w_hi[:], start=False, stop=True)
                last.then_inc(v_psum, 1)

            def score_tile(b, s):
                g = b * TILES + s
                pe.wait_ge(tlo_ready, b * 2 + s // CT + 1)
                wait(pe, exp_ready, g - 1)
                if s == 0:
                    pe.wait_ge(zlo_ready, b * 2 + 2)
                rows = ds(b * N + s * P, P)
                for half in range(2):
                    cols = ds(b * N + half * HALF, HALF)
                    dst = scores[:, s % 2, half * HALF:(half + 1) * HALF]
                    nc.tensor.matmul(dst, t_hi[:, rows], z_hi[:, cols], start=True, stop=False)
                    nc.tensor.matmul(dst, t_hi[:, rows], z_lo[:, cols], start=False, stop=False)
                    last = nc.tensor.matmul(dst, t_lo[:, rows], z_hi[:, cols], start=False, stop=True)
                last.then_inc(scores_ready, 1)

            def transposes(b, i):
                g = b * TILES + i
                for part, (src, ready, done) in enumerate(((p_hi, phi_ready, tr_hi), (p_lo, plo_ready, tr_lo))):
                    pe.wait_ge(ready, g + 1)
                    if part == 1:
                        wait(pe, ptT_lo, g)
                    elif i % 2:
                        pe.wait_ge(ptT_hi_even, b * (TILES // 2) + (i + 1) // 2)
                    else:
                        wait(pe, ptT_hi_odd, b * (TILES // 2) + i // 2)
                    for k in range(TILES):
                        last = nc.tensor.transpose(tr[:, part, k * P:(k + 1) * P],
                                                   src[:, i % RING, k * P:(k + 1) * P], ident16[:])
                    last.then_inc(done, 1)

            def pv_quarter(b, r):
                c, quarter = divmod(r, CT)
                h = b * CHUNKS + c
                if quarter == 0:
                    pe.wait_ge(ptT_hi_even, b * (TILES // 2) + (c + 1) * CT // 2)
                    pe.wait_ge(ptT_hi_odd, b * (TILES // 2) + (c + 1) * CT // 2)
                    pe.wait_ge(ptT_lo, b * TILES + (c + 1) * CT)
                    pe.wait_ge(attn_ready, h + 1)
                if c == 0 and quarter % 2 == 0:
                    pe.wait_ge(vlo_ready, b * 2 + quarter // 2 + 1)
                per = TILES // CT
                for k in range(quarter * per, (quarter + 1) * per):
                    keys = ds(b * N + k * P, P)
                    nc.tensor.matmul(pv[:], v_hi[:, keys], ptT[:, c, 0, k], start=(k == 0), stop=False)
                    nc.tensor.matmul(pv[:], v_hi[:, keys], ptT[:, c, 1, k], start=False, stop=False)
                    last = nc.tensor.matmul(pv[:], v_lo[:, keys], ptT[:, c, 0, k], start=False,
                                            stop=(k == TILES - 1))
                if quarter == CT - 1:
                    last.then_inc(pv_ready, 1)

            def pv_last():
                pe.wait_ge(ptT_hi_even, B * TILES // 2)
                pe.wait_ge(ptT_hi_odd, B * TILES // 2)
                pe.wait_ge(ptT_lo, B * TILES)
                for q in range(2):
                    cols = slice(q * HALF // 2, (q + 1) * HALF // 2)
                    dst = scores[:, q, 0:HALF // 2]
                    for k in range(TILES):
                        keys = slice((B - 1) * N + k * P, (B - 1) * N + (k + 1) * P)
                        hi, lo = ptT[:, CHUNKS - 1, 0, k, cols], ptT[:, CHUNKS - 1, 1, k, cols]
                        nc.tensor.matmul(dst, v_hi[:, keys], hi, start=(k == 0), stop=False)
                        nc.tensor.matmul(dst, v_hi[:, keys], lo, start=False, stop=False)
                        last = nc.tensor.matmul(dst, v_lo[:, keys], hi, start=False, stop=(k == TILES - 1))
                    last.then_inc(pv_ready, 1)

            def spread_inverse(b, c):
                h = b * CHUNKS + c
                pe.wait_ge(diag_ready, h * 2 + 2)
                nc.tensor.matmul(misc[:], ones16[:], diag_hi[:].rearrange("p a b -> p (a b)"), start=True, stop=False)
                nc.tensor.matmul(misc[:], ones16[:], diag_lo[:].rearrange("p a b -> p (a b)"), start=False, stop=True
                                 ).then_inc(r_psum, 1)

            pe.wait_ge(wqkv_loaded, 16)
            nc.tensor.matmul(scores[:, 0, 0:P], wqkv_sb[:, 0], wqkv_sb[:, 1], start=True, stop=True
                             ).then_inc(a_psum, 1)
            pe.wait_ge(consts, 1)
            pe.wait_ge(w_loaded, 16 * W_LOADS)
            nc.tensor.transpose(scores[:, 1, 0:P], wp_sb[:], ident32[:]).then_inc(wpT_psum, 1)
            pe.wait_ge(const_dve, 5)
            group_average(0, chan_ready, chan_mv[:, 0:1], mean_psum)
            pe.wait_ge(araw_ready, 1)
            pe.wait_ge(c_loaded, 32)
            nc.tensor.matmul(scores[:, 0, HALF:HALF + 1], a_raw[:], beta_c[:], start=True, stop=False)
            nc.tensor.matmul(scores[:, 0, HALF:HALF + 1], wqkv_sb[:, 1], bq_c[:], start=False, stop=True
                             ).then_inc(c_psum, 1)
            group_average(0, var_ready, var_in[:], var_psum)
            pe.wait_ge(wpT_ready, 1)
            nc.tensor.matmul(scores[:, 1, HALF:HALF + P], wqkv_sb[:, 2], wpT[:], start=True, stop=True
                             ).then_inc(w_psum, 1)
            pe.wait_ge(const_warm, 1)
            for _ in range(WARM_UP):
                nc.tensor.matmul(scores[:, 1, 0:HALF], ones16[:], warm[:], start=True, stop=True)

            pe.wait_ge(a_ready, 5)
            pe.wait_ge(vareps_ready, 1)
            t_products(0, 0)
            pe.wait_ge(wraw_ready, 1)
            pe.wait_ge(o_loaded, 32)
            nc.tensor.matmul(pv[:, 0:1], w_raw[:], beta_c[:], start=True, stop=False)
            nc.tensor.matmul(pv[:, 0:1], wpT[:], bv_c[:], start=False, stop=True).then_inc(bo_psum, 1)
            for _ in range(WARM_GAP):
                nc.tensor.matmul(scores[:, 1, 0:HALF], ones16[:], warm[:], start=True, stop=True)
            pe.wait_ge(wmat_ready, 1)

            def body(b, prev, cur, nxt):
                for s in range(TILES):
                    if cur:
                        score_tile(b, s)
                    if cur and not prev:
                        if s == 0:
                            t_products(b, 1)
                        if s == 3:
                            pe.wait_ge(vlo_ready, b * 2 + 1)
                            group_average(b + 1, chan_ready, chan_mv[:, 0:1], mean_psum)
                        if s == 4:
                            group_average(b + 1, var_ready, var_in[:], var_psum)
                        if s == 7:
                            pe.wait_ge(vlo_ready, b * 2 + 2)
                            t_products(b + 1, 0)
                    if prev and s < T_LAG:
                        transposes(b - 1, s + TILES - T_LAG)
                    if cur and s >= T_LAG:
                        transposes(b, s - T_LAG)
                    if cur and s == 1:
                        if prev:
                            pe.wait_ge(r_ready, b * CHUNKS - 1)
                        else:
                            pe.wait_ge(tlo_ready, b * 2 + 2)
                        if not prev:
                            pe.wait_ge(w_ready, 3)
                        v_products(b, 0)
                    if cur and s == 5:
                        if prev:
                            pe.wait_ge(r_ready, b * CHUNKS)
                        else:
                            pe.wait_ge(vareps_ready, b + 2)
                        v_products(b, 1)
                    if prev and s < (PV_LAG if cur else PV_LAG - CT):
                        pv_quarter(b - 1, s + TILES - PV_LAG)
                    if cur and s >= PV_LAG:
                        pv_quarter(b, s - PV_LAG)
                    if prev and s == 0:
                        if cur:
                            pe.wait_ge(tlo_ready, b * 2 + 2)
                        else:
                            pe.wait_ge(vlo_ready, b * 2)
                        spread_inverse(b - 1, 0)
                    if prev and nxt and s == 2:
                        pe.wait_ge(vlo_ready, b * 2 + 1)
                        group_average(b + 1, chan_ready, chan_mv[:, 0:1], mean_psum)
                    if prev and nxt and s == 3:
                        group_average(b + 1, var_ready, var_in[:], var_psum)
                    if prev and s == 4:
                        if nxt:
                            pe.wait_ge(vareps_ready, b + 2)
                        elif cur:
                            pe.wait_ge(vlo_ready, b * 2 + 1)
                        else:
                            pe.wait_ge(r_ready, b * CHUNKS - 1)
                        spread_inverse(b - 1, 1)
                    if prev and nxt and s == 6:
                        pe.wait_ge(vlo_ready, b * 2 + 2)
                        t_products(b + 1, 0)
                    if nxt and s == 7:
                        t_products(b + 1, 1)

            images(pe, body)
            pv_last()


_INS = ['x', 'L0_conv_gamma', 'L0_conv_beta', 'L0_conv_w_qkv', 'L0_conv_b_qkv', 'L0_conv_w_proj', 'L0_conv_b_proj']
_OUT = ((4, 128, 32, 32), 'float32')


def kernel(**inputs):
    import numpy as _np
    import concourse.bacc as _bacc
    from concourse import mybir as _mybir
    from concourse.bass_utils import run_bass_kernel_spmd as _run

    nc = _bacc.Bacc("TRN2", target_bir_lowering=False, num_devices=1)
    arrays, args = {}, []
    for name in _INS:
        a = _np.ascontiguousarray(inputs[name])
        arrays[f"in_{name}_dram"] = a
        args.append(nc.dram_tensor(f"in_{name}_dram", a.shape, _mybir.dt.from_np(a.dtype), kind="ExternalInput").ap())
    shape, dtype = _OUT
    out = nc.dram_tensor("out_0_dram", shape, _mybir.dt.from_np(_np.dtype(dtype)), kind="ExternalOutput").ap()
    attention_block(nc, *args, out)
    r = _run(nc, [arrays], core_ids=[0])
    return r.results[0]["out_0_dram"]
```
